# Optimizing a Trainium2 kernel written in Bass

```python
import numpy as np
import jax
import jax.numpy as jnp

def _softmax(x, axis=-1):
    return jax.nn.softmax(x, axis=axis)

def _gelu(x):
    return jax.nn.gelu(x, approximate=True)

def _silu(x):
    return jax.nn.silu(x)

def _sigmoid(x):
    return jax.nn.sigmoid(x)

def _layernorm(x, axis=-1, eps=1e-05):
    m = jnp.mean(x, axis=axis, keepdims=True)
    v = jnp.var(x, axis=axis, keepdims=True)
    return (x - m) / jnp.sqrt(v + eps)

def _scatter_add(tgt, idx, src, axis=0):
    return tgt.at[idx].add(src)

def _segment_sum(src, seg, n):
    return jax.ops.segment_sum(src, seg, n)
kernel_name = 'mk_gnn_preln_d2_gnn_r8_b5db53'

def setup_inputs(seed: int=0):
    np.random.seed(seed)
    _w = jnp.asarray

    def _rec_inputs():
        import jax
        import jax.numpy as jnp
        _gk = jax.random.key(seed)
        x = -0.0007083 + 1.001 * jax.random.normal(jax.random.fold_in(_gk, 1), (6250, 48), jnp.float32)
        _s = jax.random.randint(jax.random.fold_in(_gk, 2), (100000,), 0, 6250, jnp.int32)
        _d = jax.random.randint(jax.random.fold_in(_gk, 3), (100000,), 0, 6250, jnp.int32)
        _loop = jnp.arange(6250, dtype=jnp.int32)
        src = jnp.concatenate([_s, _d, _loop])
        dst = jnp.concatenate([_d, _s, _loop])
        _o = jnp.argsort(dst, stable=True)
        src = src[_o]
        dst = dst[_o]
        edge_attr_40 = jax.random.uniform(jax.random.fold_in(_gk, 12), (206250, 40), jnp.float32, 0.0, 1)
        edge_weight = jax.random.uniform(jax.random.fold_in(_gk, 14), (206250,), jnp.float32, 0.0, 6.99999)
        node_type_119 = jax.random.randint(jax.random.fold_in(_gk, 15), (6250,), 0, 119, jnp.int32)
        node_vec = jax.random.uniform(jax.random.fold_in(_gk, 16), (6250,), jnp.float32, 0.0, 1.49999)
        return (x, src, dst, edge_attr_40, edge_weight, node_type_119, node_vec)
    x, src, dst, edge_attr_40, edge_weight, node_type_119, node_vec = _rec_inputs()

    def _L0_gnn_setup():
        import jax, jax.numpy as jnp
        import numpy as np
        CUTOFF = 6.0
        LN_EPS = 1e-05
        key = jax.random.key(seed)
        ks = jax.random.split(key, 16)
        N, E, H, R, NEL, G = (6250, 100000, 48, 40, 119, 32)
        inp = {'h': jax.random.normal(ks[0], (N, H), jnp.float32), 'edge_index': jax.random.randint(ks[1], (2, E), 0, N, jnp.int64), 'edge_attr': jax.random.uniform(ks[2], (E, R), jnp.float32), 'distances': jax.random.uniform(ks[3], (E,), jnp.float32) * 7.0, 'atom_z': jax.random.randint(ks[4], (N,), 0, NEL, jnp.int64), 'node_mult': jax.random.uniform(ks[5], (N,), jnp.float32) + 0.5, 'batch': jnp.zeros((N,), jnp.int64), 'W1': jax.random.normal(ks[6], (H, R), jnp.float32) / np.sqrt(R), 'b1': jax.random.normal(ks[7], (H,), jnp.float32) * 0.01, 'W2': jax.random.normal(ks[8], (H, H), jnp.float32) / np.sqrt(H), 'b2': jax.random.normal(ks[9], (H,), jnp.float32) * 0.01, 'emb': jax.random.normal(ks[10], (NEL, G), jnp.float32) * 0.01, 'adaptW': jax.random.normal(ks[11], (G, G), jnp.float32) * 0.01, 'gamma': jnp.ones((H,), jnp.float32), 'beta': jnp.zeros((H,), jnp.float32)}
        return inp
    _L0_gnn_all = _L0_gnn_setup()
    _L0_gnn_in = {k: v for k, v in _L0_gnn_all.items() if k in ('W1', 'b1', 'W2', 'b2', 'emb', 'adaptW', 'gamma', 'beta')}
    del _L0_gnn_all

    def _L1_gnn_setup():
        import jax, jax.numpy as jnp
        import numpy as np
        N = 12500
        E = 200000
        D = 48
        K = 5
        ALPHA = 0.8
        key = jax.random.key(seed)
        k1, k2 = jax.random.split(key)
        x = jax.random.normal(k1, (N, D), dtype=jnp.float32)
        edge_index = jax.random.randint(k2, (2, E), 0, N, dtype=jnp.int32)
        return {'x': x, 'edge_index': edge_index}
    _L1_gnn_all = _L1_gnn_setup()
    _L1_gnn_in = {k: v for k, v in _L1_gnn_all.items() if k in ()}
    del _L1_gnn_all
    return {'x': x, 'src': src, 'dst': dst, 'edge_attr_40': edge_attr_40, 'edge_weight': edge_weight, 'node_type_119': node_type_119, 'node_vec': node_vec, 'L0_gnn_W1': _L0_gnn_in['W1'], 'L0_gnn_b1': _L0_gnn_in['b1'], 'L0_gnn_W2': _L0_gnn_in['W2'], 'L0_gnn_b2': _L0_gnn_in['b2'], 'L0_gnn_emb': _L0_gnn_in['emb'], 'L0_gnn_adaptW': _L0_gnn_in['adaptW'], 'L0_gnn_gamma': _L0_gnn_in['gamma'], 'L0_gnn_beta': _L0_gnn_in['beta']}

def reference(x, src, dst, edge_attr_40, edge_weight, node_type_119, node_vec, L0_gnn_W1, L0_gnn_b1, L0_gnn_W2, L0_gnn_b2, L0_gnn_emb, L0_gnn_adaptW, L0_gnn_gamma, L0_gnn_beta):
    import jax
    import jax.numpy as jnp

    def _L0_gnn_ref(h, edge_index, edge_attr, distances, atom_z, node_mult, batch, W1, b1, W2, b2, emb, adaptW, gamma, beta):
        import jax, jax.numpy as jnp
        import numpy as np
        CUTOFF = 6.0
        LN_EPS = 1e-05
        src, dst = (edge_index[0], edge_index[1])
        N = h.shape[0]
        gate = jax.nn.silu(edge_attr @ W1.T + b1) @ W2.T + b2
        ei = emb[atom_z[src]]
        ej = emb[atom_z[dst]]
        adapt_logit = jnp.sum(ei * (ej @ adaptW.T), axis=-1, keepdims=True)
        gate = gate + adapt_logit
        cw = jnp.where(distances < CUTOFF, 0.5 * (jnp.cos(jnp.pi * distances / CUTOFF) + 1.0), 0.0)
        mj = node_mult[dst]
        msg = gate * h[dst] * (cw * mj)[:, None]
        agg = jax.ops.segment_sum(msg, src, num_segments=N)
        tot = jax.ops.segment_sum(mj, src, num_segments=N)
        agg = agg / jnp.clip(tot, 1e-08, None)[:, None]
        x = h + agg
        mu = jnp.mean(x, axis=-1, keepdims=True)
        var = jnp.mean(jnp.square(x - mu), axis=-1, keepdims=True)
        return (x - mu) / jnp.sqrt(var + LN_EPS) * gamma + beta

    def _L1_gnn_ref(x, edge_index):
        import jax, jax.numpy as jnp
        import numpy as np
        N = 12500
        E = 200000
        D = 48
        K = 5
        ALPHA = 0.8
        n = x.shape[0]
        loops = jnp.arange(n, dtype=edge_index.dtype)
        row = jnp.concatenate([edge_index[0], loops])
        col = jnp.concatenate([edge_index[1], loops])
        deg = jax.ops.segment_sum(jnp.ones(row.shape, x.dtype), col, num_segments=n)
        dinv = jnp.where(deg > 0, jax.lax.rsqrt(deg), jnp.zeros((), x.dtype))
        w = dinv[row] * dinv[col]

        def step(h, _):
            m = jax.ops.segment_sum(w[:, None] * h[row], col, num_segments=n)
            h = (1.0 - ALPHA) * m + ALPHA * x
            return (h, None)
        h, _ = jax.lax.scan(step, x, None, length=K)
        return h
    edge_index = jnp.stack([src, dst])
    batch0 = jnp.zeros((6250,), jnp.int32)
    h = jnp.maximum(_layernorm(x, axis=-1), 0.0)
    x = x + _L0_gnn_ref(h, edge_index, edge_attr_40, edge_weight, node_type_119, node_vec, batch0, L0_gnn_W1, L0_gnn_b1, L0_gnn_W2, L0_gnn_b2, L0_gnn_emb, L0_gnn_adaptW, L0_gnn_gamma, L0_gnn_beta)
    h = jnp.maximum(_layernorm(x, axis=-1), 0.0)
    x = x + _L1_gnn_ref(h, edge_index)
    return x

_drawn_inputs = setup_inputs


def setup_inputs(seed=0):
    import zlib

    import numpy as np

    out = dict(_drawn_inputs(seed))
    spreads = {'L0_gnn_gamma': (1.0, 0.2), 'L0_gnn_beta': (0.0, 0.1)}
    factors = {'edge_attr_40': 5.208,
     'edge_weight': 4.29,
     'node_vec': 6.027,
     'L0_gnn_b1': 183.919,
     'L0_gnn_b2': 64.0,
     'L0_gnn_emb': 64.0,
     'L0_gnn_adaptW': 64.0}
    for name, (base, spread) in spreads.items():
        noise = np.random.default_rng([zlib.crc32(name.encode()), seed]).standard_normal(out[name].shape)
        drawn = base * np.exp(spread * noise) if base else spread * noise
        out[name] = jnp.asarray(drawn.astype(out[name].dtype))
    for name, factor in factors.items():
        out[name] = (out[name] * factor).astype(out[name].dtype)
    return out
```

```python
from contextlib import ExitStack

import concourse.bass as bass
from concourse import mybir

F32, I32, F16 = mybir.dt.float32, mybir.dt.int32, mybir.dt.float16
ALU, ACT, AX = mybir.AluOpType, mybir.ActivationFunctionType, mybir.AxisListType

P = 128
N, H, R, G, T, E = 6250, 48, 40, 32, 119, 206250
TILES = -(-N // P)
NPAD = TILES * P
CHUNKS = 4 * -(-E // (4 * P))
EPAD = CHUNKS * P
QUADS = CHUNKS // 4
DUMP = NPAD
ROWS = NPAD + P
W = 64
DW = 96
STEPS = 5
ALPHA = 0.8
CUTOFF = 6.0
EPS = 1e-5
PI = 3.141592653589793


def gnn_kernel(nc, x, src, dst, dist, attr_t, mult_n, types, w1t, b1, w2e, emb, emb_t, adapt_t, gamma, beta, out):
    ctx = ExitStack()
    with ctx:
        def sb(name, shape, dt=F32):
            return ctx.enter_context(nc.sbuf_tensor(name, shape, dt))

        def pb(name, shape):
            return ctx.enter_context(nc.psum_tensor(name, shape, F32))

        def sem(name):
            return ctx.enter_context(nc.semaphore(name))

        by_dst = nc.dram_tensor("by_dst", [NPAD, DW], F32, kind="Internal")
        by_src = nc.dram_tensor("by_src", [NPAD, G], F32, kind="Internal")
        u_tab = nc.dram_tensor("u_tab", [NPAD, H], F32, kind="Internal")
        sums = [nc.dram_tensor(f"sums{r}", [ROWS, W], F32, kind="Internal") for r in range(4)]

        xs = sb("xs", [P, TILES, H])
        hs_n = sb("hs_n", [P, TILES, H])
        tmp = sb("tmp", [P, TILES, H])
        acc = sb("acc", [P, TILES, H])
        part = sb("part", [P, 4, TILES, H + 1])
        row = sb("row", [P, TILES, 1])
        row2 = sb("row2", [P, TILES, 1])
        rstd = sb("rstd", [P, TILES, 1])
        mult = sb("mult", [P, TILES, 1])
        deg = sb("deg", [P, TILES, 1])
        dinv = sb("dinv", [P, TILES, 1])
        fifth = sb("fifth", [P, TILES, 1])
        gam = sb("gam", [P, H])
        bet = sb("bet", [P, H])
        zt = sb("zt", [T, NPAD], I32)
        zhot = zt[:].bitcast(F32)
        pidx = sb("pidx", [P, 1], I32)
        pidx_f = sb("pidx_f", [P, 1])
        dump = sb("dump", [P, 4])
        etab = sb("etab", [T, 2 * G])
        embT = sb("embT", [G, T])
        adT = sb("adT", [G, G])
        zz = sb("zz", [P, TILES, 2 * G])
        x0s = zz[:].rearrange("p t c -> p (t c)")[:, 0:TILES * H].rearrange("p (t c) -> p t c", c=H)
        drow = sb("drow", [P, TILES, DW])
        src_i = sb("src_i", [P, CHUNKS], I32)
        dst_i = sb("dst_i", [P, CHUNKS], I32)
        src_f = sb("src_f", [P, CHUNKS])
        dst_f = sb("dst_f", [P, CHUNKS])
        dis = sb("dis", [P, CHUNKS])
        cut = sb("cut", [P, CHUNKS])
        act_in = sb("act_in", [P, CHUNKS])
        zero = sb("zero", [P, (ROWS // P) * W])
        ones = sb("ones", [P, 1])
        eps = sb("eps", [P, 1])
        ident = sb("ident", [P, P])
        tri = sb("tri", [P, P])
        w1s = sb("w1s", [R, H])
        b1s = sb("b1s", [H, 1])
        w2s = sb("w2s", [H + 1, H])
        attr_sb = sb("attr_sb", [R, 4 * P])
        hid = sb("hid", [H + 1, 4 * P])
        gi_d = sb("gi_d", [P, 4], I32)
        gi_s = sb("gi_s", [P, 4], I32)
        seg = sb("seg", [P, 4])
        dg = sb("dg", [P, 4, DW])
        sg = sb("sg", [P, 4, G])
        ug = sb("ug", [P, 4, H])
        same = sb("same", [P, 4, P])
        before = sb("before", [P, 4, P])
        nbef = sb("nbef", [P, 4])
        away = sb("away", [P, 4])
        sidx = sb("sidx", [P, 4], I32)
        hmc = sb("hmc", [P, 4, H])
        ad = sb("ad", [P, 4, G])
        ads = sb("ads", [P, 4, 1])
        gate_a = sb("gate_a", [P, 4, H])
        msg = sb("msg", [P, 4, H + 1])
        outrow = sb("outrow", [P, 4, W])

        ps_seg = pb("ps_seg", [P, 4, P])
        ps_h = pb("ps_h", [P, 512])
        ps_gate = pb("ps_gate", [P, 4, H])
        ps_sum = pb("ps_sum", [P, 4, H + 1])
        ps_z = pb("ps_z", [P, 7, 2 * G])
        ps_e = pb("ps_e", [P, 512])

        loads = ["x", "mult", "gam", "bet", "zt", "embT", "adT", "emb", "src", "dst", "dis", "w1", "b1", "w2"]
        s_load = sem("s_load")
        s_const = sem("s_const")
        s_zero = sem("s_zero")
        s_var = sem("s_var")
        s_sqrt = sem("s_sqrt")
        s_ang = sem("s_ang")
        s_sin = sem("s_sin")
        s_e2 = sem("s_e2")
        s_e2c = sem("s_e2c")
        s_z = sem("s_z")
        s_zc = sem("s_zc")
        s_rows = sem("s_rows")
        s_tab = sem("s_tab")
        s_dve = sem("s_dve")
        a_idx, a_seg, a_at, a_h, a_hid, a_gate, a_gath, a_msg, a_sum, a_out, a_dve, a_mg = (
            sem("a_" + n) for n in ("idx", "seg", "at", "h", "hid", "gate", "gath", "msg", "sum", "out", "dve", "mg"))
        b_idx, b_seg, b_eq, b_sum, b_out, b_dve = (
            sem("b_" + n) for n in ("idx", "seg", "eq", "sum", "out", "dve"))
        b_gath = [sem(f"b_gath{p}") for p in range(STEPS + 1)]
        b_add = [sem(f"b_add{p}") for p in range(STEPS + 1)]
        s_add = sem("s_add")
        s_mark = sem("s_mark")
        s_turn = sem("s_turn")
        s_back = sem("s_back")
        b_back = sem("b_back")
        b_used = sem("b_used")
        b_u = sem("b_u")
        b_rez = sem("b_rez")
        s_fin = sem("s_fin")
        s_outd = sem("s_outd")

        block = ctx.enter_context(nc.Block())
        tiles = lambda ap: ap.rearrange("(t p) c -> p t c", p=P)
        L1PASSES = STEPS + 1

        @block.sync
        def _(sp):
            sp.dma_start(xs[:], tiles(x)).then_inc(s_load, 16)
            sp.dma_start(mult[:, :, 0], mult_n).then_inc(s_load, 16)
            sp.dma_start(gam[:], gamma.partition_broadcast(P)).then_inc(s_load, 16)
            sp.dma_start(bet[:], beta.partition_broadcast(P)).then_inc(s_load, 16)
            sp.dma_start(zt[:], types.partition_broadcast(T)).then_inc(s_load, 16)
            sp.dma_start(embT[:], emb_t).then_inc(s_load, 16)
            sp.dma_start(adT[:], adapt_t).then_inc(s_load, 16)
            sp.dma_start(etab[:, 0:G], emb).then_inc(s_load, 16)
            sp.dma_start(src_i[:], src).then_inc(s_load, 16)
            sp.dma_start(dst_i[:], dst).then_inc(s_load, 16)
            sp.dma_start(dis[:], dist).then_inc(s_load, 16)
            sp.dma_start(w1s[:], w1t).then_inc(s_load, 16)
            sp.dma_start(b1s[:], b1).then_inc(s_load, 16)
            sp.dma_start(w2s[:], w2e).then_inc(s_load, 16)
            sp.wait_ge(s_rows, 2)
            sp.dma_start(tiles(by_dst[:, :]), drow[:]).then_inc(s_tab, 16)
            sp.dma_start(tiles(by_src[:, :]), zz[:, :, 0:G]).then_inc(s_tab, 16)
            sp.dma_start(tiles(u_tab[:, :]), tmp[:]).then_inc(s_tab, 16)
            with sp.Fori(0, QUADS) as q:
                sp.wait_ge(a_idx, q + 1)
                sp.dma_start(attr_sb[:], attr_t[:, bass.ds(q * (4 * P), 4 * P)]).then_inc(a_at, 16)
            sp.wait_ge(s_add, 64 * (QUADS + 1))
            for r in range(4):
                sp.dma_start(part[:, r], tiles(sums[r][0:NPAD, 0:H + 1])).then_inc(s_back, 16)
            for p in range(L1PASSES):
                sp.wait_ge(b_add[p], 64 * (QUADS + 1))
                for r in range(4):
                    sp.dma_start(part[:, r, :, 0:H], tiles(sums[r][0:NPAD, 0:H])).then_inc(b_back, 16)
                sp.wait_ge(b_used, p + 1)
                sp.dma_start(tiles(u_tab[:, :]), acc[:]).then_inc(b_u, 16)
            sp.wait_ge(b_u, 16 * L1PASSES)
            sp.wait_ge(s_fin, 1)
            sp.dma_start(tiles(out), xs[:]).then_inc(s_outd, 16)
            sp.wait_ge(s_outd, 16)

        @block.gpsimd
        def _(pool):
            pool.iota(pidx[:], [[0, 1]], base=0, channel_multiplier=1).then_inc(s_const, 1)
            pool.memset(ident[:], 0.0).then_inc(s_const, 1)
            pool.memset(tri[:], 1.0).then_inc(s_const, 1)
            pool.wait_ge(s_const, 3)
            pool.affine_select(out=ident[:], in_=ident[:], compare_op=ALU.not_equal, fill=1.0, base=0,
                               pattern=[[-1, P]], channel_multiplier=1).then_inc(s_const, 1)
            pool.affine_select(out=tri[:], in_=tri[:], compare_op=ALU.is_gt, fill=0.0, base=0,
                               pattern=[[-1, P]], channel_multiplier=1).then_inc(s_const, 1)

            def zero_sums(signal):
                for r in range(4):
                    pool.dma_start(sums[r].rearrange("(p t) c -> p (t c)", p=P), zero[:]).then_inc(signal, 16)

            pool.wait_ge(s_zero, 1)
            zero_sums(s_add)
            pool.wait_ge(s_tab, 48)
            with pool.Fori(0, QUADS) as q:
                pool.wait_ge(a_idx, q + 1)
                pool.sem_inc(s_mark, 1)
                for c in range(4):
                    pool.indirect_dma_start(dg[:, c, :], None, by_dst[:, :],
                                            bass.IndirectOffsetOnAxis(ap=gi_d[:, c:c + 1], axis=0)).then_inc(a_gath, 16)
                    pool.indirect_dma_start(sg[:, c, :], None, by_src[:, :],
                                            bass.IndirectOffsetOnAxis(ap=gi_s[:, c:c + 1], axis=0)).then_inc(a_gath, 16)
                pool.wait_ge(a_out, q + 1)
                pool.sem_inc(s_mark, 1)
                for c in range(4):
                    pool.indirect_dma_start(sums[c][:, :], bass.IndirectOffsetOnAxis(ap=sidx[:, c:c + 1], axis=0),
                                            outrow[:, c, :], None, compute_op=ALU.add).then_inc(s_add, 16)
            pool.wait_ge(s_back, 64)
            for p in range(L1PASSES):
                zero_sums(b_add[p])
                with pool.Fori(0, QUADS) as q:
                    n = q + p * QUADS
                    pool.wait_ge(b_idx, n + 1)
                    pool.sem_inc(s_mark, 1)
                    for c in range(4):
                        pool.indirect_dma_start(ug[:, c, :], None, u_tab[:, :],
                                                bass.IndirectOffsetOnAxis(ap=gi_s[:, c:c + 1], axis=0)).then_inc(b_gath[p], 16)
                    pool.wait_ge(b_out, n + 1)
                    pool.sem_inc(s_mark, 1)
                    for c in range(4):
                        pool.indirect_dma_start(sums[c][:, :], bass.IndirectOffsetOnAxis(ap=sidx[:, c:c + 1], axis=0),
                                                outrow[:, c, :], None, compute_op=ALU.add).then_inc(b_add[p], 16)
                pool.wait_ge(b_u, (p + 1) * 16)
                pool.sem_inc(s_mark, 1)

        @block.scalar
        def _(act):
            act.wait_ge(s_ang, 1)
            nc.scalar.activation(act_in[:], dis[:], ACT.Sin).then_inc(s_sin, 1)
            act.wait_ge(s_var, 1)
            nc.scalar.activation(rstd[:], row2[:], ACT.Sqrt, bias=eps[:]).then_inc(s_sqrt, 1)
            with act.Fori(0, QUADS) as q:
                act.wait_ge(a_h, q + 1)
                nc.scalar.activation(hid[0:H, :], ps_h[0:H, :], ACT.Silu, bias=b1s[:]).then_inc(a_hid, 1)
                act.wait_ge(a_sum, q + 1)
                nc.scalar.activation(outrow[:, :, 0:H + 1], ps_sum[:], ACT.Copy).then_inc(a_out, 1)
            for k in range(2):
                act.wait_ge(s_var, 2 + k)
                nc.scalar.activation(rstd[:], row2[:], ACT.Sqrt, bias=eps[:]).then_inc(s_sqrt, 1)
            with act.Fori(0, QUADS) as q:
                act.wait_ge(b_sum, q + 1)
                nc.scalar.activation(outrow[:, :, 0:H], ps_sum[:, :, 0:H], ACT.Copy).then_inc(b_out, 1)
            act.wait_ge(s_var, 4)
            nc.scalar.activation(dinv[:], deg[:], ACT.Sqrt).then_inc(s_sqrt, 1)
            with act.Fori(QUADS, L1PASSES * QUADS) as n:
                act.wait_ge(b_sum, n + 1)
                nc.scalar.activation(outrow[:, :, 0:H], ps_sum[:, :, 0:H], ACT.Copy).then_inc(b_out, 1)

        @block.tensor
        def _(pe):
            pe.wait_ge(s_load, 16 * len(loads))
            pe.wait_ge(s_const, 5)
            nc.tensor.matmul(ps_e[0:T, 0:G], embT[:], adT[:], start=True, stop=True).then_inc(s_e2, 1)
            pe.wait_ge(s_e2c, 1)
            for k in range(TILES // 7):
                if k:
                    pe.wait_ge(s_zc, k)
                for j in range(7):
                    t = 7 * k + j
                    last = nc.tensor.matmul(ps_z[:, j, :], zhot[:, t * P:(t + 1) * P], etab[:], start=True, stop=True)
                last.then_inc(s_z, 1)

            def ids_across(ready, count, done):
                pe.wait_ge(ready, count)
                for c in range(4):
                    last = nc.tensor.matmul(ps_seg[:, c, :], seg[:, c:c + 1].to_broadcast([P, P]), ident[:],
                                            start=True, stop=True)
                last.then_inc(done, 1)

            with pe.Fori(0, QUADS) as q:
                ids_across(a_idx, q + 1, a_seg)
                pe.wait_ge(a_at, 16 * q + 16)
                pe.sem_inc(s_turn, 1)
                nc.tensor.matmul(ps_h[0:H, :], w1s[:], attr_sb[:], start=True, stop=True).then_inc(a_h, 1)
                pe.wait_ge(a_hid, q + 1)
                for c in range(4):
                    last = nc.tensor.matmul(ps_gate[:, c, :], hid[:, c * P:(c + 1) * P], w2s[:], start=True, stop=True)
                last.then_inc(a_gate, 1)
                pe.wait_ge(a_msg, q + 1)
                for c in range(4):
                    last = nc.tensor.matmul(ps_sum[:, c, :], same[:, c, :], msg[:, c, :], start=True, stop=True)
                last.then_inc(a_sum, 1)
            for p in range(L1PASSES):
                with pe.Fori(0, QUADS) as q:
                    n = q + p * QUADS
                    ids_across(b_idx, n + 1, b_seg)
                    pe.wait_ge(b_eq, n + 1)
                    pe.wait_ge(b_gath[p], 64 * q + 64)
                    for c in range(4):
                        last = nc.tensor.matmul(ps_sum[:, c, 0:H], same[:, c, :], ug[:, c, :], start=True, stop=True)
                    last.then_inc(b_sum, 1)

        @block.vector
        def _(dve):
            V = nc.vector
            count = [0]

            def link(ins):
                count[0] += 1
                ins.then_inc(s_dve, 1)
                dve.wait_ge(s_dve, count[0])

            nv = [0]

            def layernorm_relu(dst_ap, scale_shift=None):
                link(V.tensor_reduce(row[:, :, 0], tmp[:], AX.X, ALU.add))
                link(V.tensor_scalar(row[:], row[:], 1.0 / H, None, ALU.mult))
                link(V.tensor_tensor(dst_ap, tmp[:], row[:].to_broadcast([P, TILES, H]), ALU.subtract))
                link(V.tensor_tensor(tmp[:], dst_ap, dst_ap, ALU.mult))
                link(V.tensor_reduce(row[:, :, 0], tmp[:], AX.X, ALU.add))
                nv[0] += 1
                V.tensor_scalar(row2[:], row[:], 1.0 / H, None, ALU.mult).then_inc(s_var, 1)
                dve.wait_ge(s_sqrt, nv[0])
                link(V.reciprocal(row2[:], rstd[:]))
                link(V.tensor_tensor(dst_ap, dst_ap, row2[:].to_broadcast([P, TILES, H]), ALU.mult))
                if scale_shift:
                    g_, b_ = scale_shift
                    link(V.tensor_tensor(dst_ap, dst_ap, g_[:].unsqueeze(1).to_broadcast([P, TILES, H]), ALU.mult))
                    link(V.tensor_tensor(dst_ap, dst_ap, b_[:].unsqueeze(1).to_broadcast([P, TILES, H]), ALU.add))
                else:
                    link(V.tensor_scalar(dst_ap, dst_ap, 0.0, None, ALU.max))

            V.memset(zero[:], 0.0).then_inc(s_zero, 1)
            V.memset(eps[:], EPS)
            V.memset(hid[:], 1.0)
            V.memset(drow[:], 0.0)
            link(V.memset(outrow[:], 0.0))
            dve.wait_ge(s_load, 16 * len(loads))
            dve.wait_ge(s_const, 5)
            V.tensor_scalar(cut[:], dis[:], CUTOFF, 0.5, ALU.is_lt, ALU.mult)
            link(V.tensor_scalar(act_in[:], dis[:], CUTOFF, None, ALU.min))
            V.tensor_scalar(dis[:], act_in[:], -PI / CUTOFF, PI / 2, ALU.mult, ALU.add).then_inc(s_ang, 1)
            V.tensor_copy(src_f[:], src_i[:])
            V.tensor_copy(dst_f[:], dst_i[:])
            link(V.tensor_copy(pidx_f[:], pidx[:]))
            dve.wait_ge(s_sin, 1)
            link(V.tensor_scalar(act_in[:], act_in[:], 1.0, None, ALU.add))
            link(V.tensor_tensor(cut[:], cut[:], act_in[:], ALU.mult))
            for c in range(4):
                link(V.tensor_scalar(dump[:, c:c + 1], pidx_f[:], float(DUMP), None, ALU.add))
            link(V.tensor_scalar(zhot, zt[:], float(T - 1), None, ALU.min))
            link(V.tensor_scalar(zhot, zhot, pidx_f[0:T, :], None, ALU.is_equal))
            dve.wait_ge(s_e2, 1)
            V.tensor_copy(etab[:, G:2 * G], ps_e[0:T, 0:G]).then_inc(s_e2c, 1)
            link(V.tensor_copy(tmp[:], xs[:]))
            layernorm_relu(hs_n[:])
            V.tensor_tensor(drow[:, :, 0:H], hs_n[:], mult[:].to_broadcast([P, TILES, H]), ALU.mult)
            V.tensor_copy(drow[:, :, H + G:H + G + 1], mult[:])
            for k in range(TILES // 7):
                dve.wait_ge(s_z, k + 1)
                V.tensor_copy(zz[:, 7 * k:7 * k + 7, :], ps_z[:]).then_inc(s_zc, 1)
            dve.wait_ge(s_zc, TILES // 7)
            V.tensor_copy(drow[:, :, H:H + G], zz[:, :, G:2 * G]).then_inc(s_rows, 1)
            V.memset(tmp[:], 1.0).then_inc(s_rows, 1)

            def gather_ids(sums_zeroed_or_added, value, col, by_dst_too, segments, ready):
                dve.wait_ge(sums_zeroed_or_added, value)
                V.tensor_copy(gi_s[:], src_f[:, bass.ds(col, 4)])
                if by_dst_too:
                    V.tensor_copy(gi_d[:], dst_f[:, bass.ds(col, 4)])
                V.tensor_copy(seg[:], segments[:, bass.ds(col, 4)]).then_inc(ready, 1)

            def merge(seg_across, n, chain, base, eq_ready=None):
                dve.wait_ge(seg_across, n + 1)
                dve.wait_ge(ready_of[chain], n + 1)
                ins = V.tensor_tensor(same[:], ps_seg[:], seg[:].unsqueeze(2).to_broadcast([P, 4, P]), ALU.is_equal)
                ins.then_inc(chain, 1)
                V.tensor_tensor(away[:], dump[:], seg[:], ALU.subtract)
                dve.wait_ge(chain, base + 1)
                if eq_ready is not None:
                    V.tensor_tensor(before[:], same[:], tri[:].unsqueeze(1).to_broadcast([P, 4, P]), ALU.mult).then_inc(chain, 1)
                else:
                    V.tensor_tensor(before[:], same[:], tri[:].unsqueeze(1).to_broadcast([P, 4, P]), ALU.mult).then_inc(chain, 1)
                dve.wait_ge(chain, base + 2)
                V.tensor_reduce(nbef[:], before[:], AX.X, ALU.add).then_inc(chain, 1)
                dve.wait_ge(chain, base + 3)
                V.tensor_scalar(nbef[:], nbef[:], 0.0, None, ALU.is_gt).then_inc(chain, 1)
                dve.wait_ge(chain, base + 4)
                V.tensor_tensor(away[:], away[:], nbef[:], ALU.mult).then_inc(chain, 1)
                dve.wait_ge(chain, base + 5)
                ins = V.tensor_tensor(sidx[:], away[:], seg[:], ALU.add)
                if eq_ready is not None:
                    ins.then_inc(eq_ready, 1)

            ready_of = {a_dve: a_idx, b_dve: b_idx}
            with dve.Fori(0, QUADS) as q:
                col = dve.snap(q * 4)
                gather_ids(s_add, q * 64 + 64, col, True, src_f, a_idx)
                merge(a_seg, q, a_dve, q * 7)
                dve.wait_ge(a_gath, q * 128 + 128)
                V.tensor_tensor(hmc[:], dg[:, :, 0:H], cut[:, bass.ds(col, 4)].unsqueeze(2).to_broadcast([P, 4, H]), ALU.mult)
                V.tensor_copy(msg[:, :, H:H + 1], dg[:, :, H + G:H + G + 1])
                V.tensor_tensor(ad[:], sg[:], dg[:, :, H:H + G], ALU.mult).then_inc(a_dve, 1)
                dve.wait_ge(a_dve, q * 7 + 6)
                V.tensor_reduce(ads[:, :, 0], ad[:], AX.X, ALU.add).then_inc(a_dve, 1)
                dve.wait_ge(a_dve, q * 7 + 7)
                dve.wait_ge(a_gate, q + 1)
                V.tensor_tensor(gate_a[:], ps_gate[:], ads[:].to_broadcast([P, 4, H]), ALU.add).then_inc(a_mg, 1)
                dve.wait_ge(a_mg, q + 1)
                V.tensor_tensor(msg[:, :, 0:H], gate_a[:], hmc[:], ALU.mult).then_inc(a_msg, 1)

            dve.wait_ge(s_back, 64)
            link(V.tensor_tensor(part[:, 0], part[:, 0], part[:, 1], ALU.add))
            link(V.tensor_tensor(part[:, 2], part[:, 2], part[:, 3], ALU.add))
            link(V.tensor_tensor(part[:, 0], part[:, 0], part[:, 2], ALU.add))
            link(V.tensor_scalar(row[:], part[:, 0, :, H:H + 1], 1e-8, None, ALU.max))
            link(V.reciprocal(row2[:], row[:]))
            link(V.tensor_tensor(tmp[:], part[:, 0, :, 0:H], row2[:].to_broadcast([P, TILES, H]), ALU.mult))
            link(V.tensor_tensor(tmp[:], tmp[:], hs_n[:], ALU.add))
            layernorm_relu(acc[:], (gam, bet))
            link(V.tensor_tensor(xs[:], xs[:], acc[:], ALU.add))
            link(V.tensor_copy(tmp[:], xs[:]))
            layernorm_relu(hs_n[:])

            def edge_pass(p):
                with dve.Fori(0, QUADS) as q:
                    n = q + p * QUADS
                    col = dve.snap(q * 4)
                    gather_ids(b_add[p], q * 64 + 64, col, False, dst_f, b_idx)
                    merge(b_seg, n, b_dve, n * 5, b_eq)

            def fold():
                link(V.tensor_tensor(part[:, 0], part[:, 0], part[:, 1], ALU.add))
                link(V.tensor_tensor(part[:, 2], part[:, 2], part[:, 3], ALU.add))
                link(V.tensor_tensor(part[:, 0], part[:, 0], part[:, 2], ALU.add))

            edge_pass(0)
            dve.wait_ge(b_back, 64)
            fold()
            V.tensor_scalar(deg[:], part[:, 0, :, 0:1], 1.0, None, ALU.add).then_inc(s_var, 1)
            dve.wait_ge(s_sqrt, 4)
            link(V.reciprocal(row[:], dinv[:]))
            link(V.tensor_copy(dinv[:], row[:]))
            link(V.reciprocal(fifth[:], deg[:]))
            link(V.tensor_scalar(fifth[:], fifth[:], 1.0 - ALPHA, None, ALU.mult))
            link(V.tensor_tensor(acc[:], hs_n[:], dinv[:].to_broadcast([P, TILES, H]), ALU.mult))
            V.tensor_scalar(x0s, acc[:], ALPHA, None, ALU.mult).then_inc(b_used, 1)
            for p in range(1, L1PASSES):
                edge_pass(p)
                dve.wait_ge(b_back, 64 * (p + 1))
                dve.wait_ge(b_u, 16 * p)
                fold()
                link(V.tensor_tensor(acc[:], acc[:], part[:, 0, :, 0:H], ALU.add))
                link(V.tensor_tensor(acc[:], acc[:], fifth[:].to_broadcast([P, TILES, H]), ALU.mult))
                V.tensor_tensor(acc[:], acc[:], x0s, ALU.add).then_inc(b_used, 1)
            dve.wait_ge(b_used, STEPS + 1)
            link(V.tensor_tensor(row[:], deg[:], dinv[:], ALU.mult))
            link(V.tensor_tensor(tmp[:], acc[:], row[:].to_broadcast([P, TILES, H]), ALU.mult))
            V.tensor_tensor(xs[:], xs[:], tmp[:], ALU.add).then_inc(s_fin, 1)


def kernel(x, src, dst, edge_attr_40, edge_weight, node_type_119, node_vec, L0_gnn_W1, L0_gnn_b1, L0_gnn_W2,
           L0_gnn_b2, L0_gnn_emb, L0_gnn_adaptW, L0_gnn_gamma, L0_gnn_beta):
    import numpy as np
    import concourse.bacc as bacc
    from concourse.bass_utils import run_bass_kernel_spmd

    def padded(a, n, value=0):
        a = np.asarray(a)
        return np.concatenate([a, np.full((n - a.shape[0],) + a.shape[1:], value, a.dtype)])

    def by_chunk(a, value):
        return np.ascontiguousarray(padded(a, EPAD, value).reshape(CHUNKS, P).T)

    arrays = {
        "x": padded(x, NPAD),
        "src": by_chunk(src, NPAD - 1),
        "dst": by_chunk(dst, NPAD - 1),
        "dist": by_chunk(edge_weight, 2 * CUTOFF),
        "attr_t": np.ascontiguousarray(padded(edge_attr_40, EPAD).T),
        "mult_n": np.ascontiguousarray(padded(node_vec, NPAD).reshape(TILES, P).T),
        "types": padded(node_type_119, NPAD),
        "w1t": np.ascontiguousarray(np.asarray(L0_gnn_W1).T),
        "b1": np.asarray(L0_gnn_b1).reshape(H, 1),
        "w2e": np.concatenate([np.asarray(L0_gnn_W2).T, np.asarray(L0_gnn_b2).reshape(1, H)]),
        "emb": np.asarray(L0_gnn_emb),
        "emb_t": np.ascontiguousarray(np.asarray(L0_gnn_emb).T),
        "adapt_t": np.ascontiguousarray(np.asarray(L0_gnn_adaptW).T),
        "gamma": np.asarray(L0_gnn_gamma),
        "beta": np.asarray(L0_gnn_beta),
    }
    nc = bacc.Bacc("TRN2", target_bir_lowering=False, num_devices=1)
    maps = {f"in_{n}": np.ascontiguousarray(a) for n, a in arrays.items()}
    args = [nc.dram_tensor(f"in_{n}", a.shape, mybir.dt.from_np(a.dtype), kind="ExternalInput").ap() for n, a in arrays.items()]
    out = nc.dram_tensor("out_0", (NPAD, H), F32, kind="ExternalOutput").ap()
    gnn_kernel(nc, *args, out)
    r = run_bass_kernel_spmd(nc, [maps], core_ids=[0])
    return r.results[0]["out_0"][:N]
```

```python
from contextlib import ExitStack

import concourse.bass as bass
from concourse import mybir

F32, I32, F16 = mybir.dt.float32, mybir.dt.int32, mybir.dt.float16
ALU, ACT, AX = mybir.AluOpType, mybir.ActivationFunctionType, mybir.AxisListType

P = 128
N, H, R, G, T, E = 6250, 48, 40, 32, 119, 206250
TILES = -(-N // P)
NPAD = TILES * P
CHUNKS = 4 * -(-E // (4 * P))
EPAD = CHUNKS * P
QUADS = CHUNKS // 4
DUMP = NPAD
ROWS = NPAD + P
W = 64
DW = 96
STEPS = 5
GD = 8
GCOLS = GD * TILES
GROUPS = NPAD // GD
GPB = P // GD
GT = -(-GROUPS // P)
RE = 32
WROWS = 12
WCH = WROWS * RE // P
ROWS_E = EPAD // RE
EROWS = ROWS_E + 16
EXACT = 15
SCALE = 4096.0
RING = 7
F8, U8 = mybir.dt.float8e4, mybir.dt.uint8
ALPHA = 0.8
CUTOFF = 6.0
EPS = 1e-5
PI = 3.141592653589793


def gnn_kernel(nc, x, src, dst, dist, attr_t, mult_n, types, w1t, b1, w2e, emb, emb_t, adapt_t, gamma, beta,
               edge_rows, dst_first, out):
    ctx = ExitStack()
    with ctx:
        stage = [ctx]

        def sb(name, shape, dt=F32):
            return stage[0].enter_context(nc.sbuf_tensor(name, shape, dt))

        def pb(name, shape):
            return stage[0].enter_context(nc.psum_tensor(name, shape, F32))

        def sem(name):
            return ctx.enter_context(nc.semaphore(name))

        def tiles(ap):
            return ap.rearrange("(t p) c -> p t c", p=P)

        by_dst = nc.dram_tensor("by_dst", [NPAD, DW], F32, kind="Internal")
        by_src = nc.dram_tensor("by_src", [NPAD, G], F32, kind="Internal")
        u_tab = nc.dram_tensor("u_tab", [NPAD, H], F32, kind="Internal")
        sums = [nc.dram_tensor(f"sums{r}", [ROWS, W], F32, kind="Internal") for r in range(4)]
        counts_d = nc.dram_tensor("counts_d", [TILES, P, TILES * P], U8, kind="Internal")

        xs = sb("xs", [P, TILES, H])
        hs_n = sb("hs_n", [P, TILES, H])
        row = sb("row", [P, TILES, 1])
        row2 = sb("row2", [P, TILES, 1])
        deg = sb("deg", [P, TILES, 1])
        dinv = sb("dinv", [P, TILES, 1])
        fifth = sb("fifth", [P, TILES, 1])
        gam = sb("gam", [P, H])
        bet = sb("bet", [P, H])
        pidx = sb("pidx", [P, 1], I32)
        pidx_f = sb("pidx_f", [P, 1])
        dump = sb("dump", [P, 4])
        src_f = sb("src_f", [P, CHUNKS])
        dst_f = sb("dst_f", [P, CHUNKS])
        eps = sb("eps", [P, 1])
        ident = sb("ident", [P, P])
        tri = sb("tri", [P, P])
        dense = sb("dense", [1, 1], I32)

        loads = ["x", "mult", "gam", "bet", "zt", "embT", "adT", "emb", "src", "dst", "dis", "w1", "b1", "w2"]
        s_load = sem("s_load")
        s_const = sem("s_const")
        s_zero = sem("s_zero")
        s_var = sem("s_var")
        s_sqrt = sem("s_sqrt")
        s_ang = sem("s_ang")
        s_sin = sem("s_sin")
        s_e2 = sem("s_e2")
        s_e2c = sem("s_e2c")
        s_z = sem("s_z")
        s_zc = sem("s_zc")
        s_rows = sem("s_rows")
        s_tab = sem("s_tab")
        s_dve = sem("s_dve")
        a_idx, a_seg, a_at, a_h, a_hid, a_gate, a_gath, a_msg, a_sum, a_out, a_dve, a_mg = (
            sem("a_" + n) for n in ("idx", "seg", "at", "h", "hid", "gate", "gath", "msg", "sum", "out", "dve", "mg"))
        b_idx, b_seg, b_eq, b_sum, b_out, b_dve = (
            sem("b_" + n) for n in ("idx", "seg", "eq", "sum", "out", "dve"))
        b_gath = [sem(f"b_gath{p}") for p in range(STEPS + 1)]
        b_add = [sem(f"b_add{p}") for p in range(STEPS + 1)]
        s_add = sem("s_add")
        s_mark = sem("s_mark")
        s_turn = sem("s_turn")
        s_go = sem("s_go")
        s_back = sem("s_back")
        b_back = sem("b_back")
        b_used = sem("b_used")
        b_u = sem("b_u")
        b_rez = sem("b_rez")
        c_load, c_row, c_idx, c_win, c_key, c_tr, c_trc, c_dve, c_one, c_used, c_cnt, c_took, c_free, c_deg, c_degc, c_sum = (
            sem("c_" + n) for n in ("load", "row", "idx", "win", "key", "tr", "trc", "dve", "one", "used", "cnt", "took",
                                    "free", "deg", "degc", "sum"))
        c_stored = [sem(f"c_stored{k}") for k in range(2)]
        c_over, c_over2 = sem("c_over"), sem("c_over2")
        c_turn, c_mark, c_io = sem("c_turn"), sem("c_mark"), sem("c_io")
        d_in = [sem(f"d_in{j}") for j in range(RING)]
        d_sum, d_lo, d_bank = ([sem(f"d_{n}{k}") for k in range(2)] for n in ("sum", "lo", "bank"))
        d_free, d_u, d_turn, d_dve, d_sq, d_ac = (sem("d_" + n) for n in ("free", "u", "turn", "dve", "sq", "ac"))
        s_fin = sem("s_fin")
        s_outd = sem("s_outd")


        count = [0]

        def dve_link(dve, ins):
            count[0] += 1
            ins.then_inc(s_dve, 1)
            dve.wait_ge(s_dve, count[0])

        def gather_ids(dve, bufs, sums_zeroed_or_added, value, col, by_dst_too, segments, ready):
            gi_s, gi_d, seg = bufs[0:3]
            V = nc.vector
            dve.wait_ge(sums_zeroed_or_added, value)
            V.tensor_copy(gi_s[:], src_f[:, bass.ds(col, 4)])
            if by_dst_too:
                V.tensor_copy(gi_d[:], dst_f[:, bass.ds(col, 4)])
            V.tensor_copy(seg[:], segments[:, bass.ds(col, 4)]).then_inc(ready, 1)

        def merge(dve, bufs, seg_across, n, chain, base, ids_ready, eq_ready):
            _, _, seg, same, before, nbef, away, sidx, ps_seg = bufs
            V = nc.vector
            dve.wait_ge(seg_across, n + 1)
            dve.wait_ge(ids_ready, n + 1)
            V.tensor_tensor(same[:], ps_seg[:], seg[:].unsqueeze(2).to_broadcast([P, 4, P]), ALU.is_equal).then_inc(chain, 1)
            V.tensor_tensor(away[:], dump[:], seg[:], ALU.subtract)
            dve.wait_ge(chain, base + 1)
            V.tensor_tensor(before[:], same[:], tri[:].unsqueeze(1).to_broadcast([P, 4, P]), ALU.mult).then_inc(chain, 1)
            dve.wait_ge(chain, base + 2)
            V.tensor_reduce(nbef[:], before[:], AX.X, ALU.add).then_inc(chain, 1)
            dve.wait_ge(chain, base + 3)
            V.tensor_scalar(nbef[:], nbef[:], 0.0, None, ALU.is_gt).then_inc(chain, 1)
            dve.wait_ge(chain, base + 4)
            V.tensor_tensor(away[:], away[:], nbef[:], ALU.mult).then_inc(chain, 1)
            dve.wait_ge(chain, base + 5)
            ins = V.tensor_tensor(sidx[:], away[:], seg[:], ALU.add)
            if eq_ready is not None:
                ins.then_inc(eq_ready, 1)

        def ids_across(pe, ps_seg, seg, ready, n, done):
            pe.wait_ge(ready, n)
            for c in range(4):
                last = nc.tensor.matmul(ps_seg[:, c, :], seg[:, c:c + 1].to_broadcast([P, P]), ident[:],
                                        start=True, stop=True)
            last.then_inc(done, 1)

        def zero_sums(pool, zero, signal):
            for r in range(4):
                pool.dma_start(sums[r].rearrange("(p t) c -> p (t c)", p=P), zero[:]).then_inc(signal, 16)

        with ExitStack() as st:
            stage[0] = st
            tmp = sb("tmp", [P, TILES, H])
            acc = sb("acc", [P, TILES, H])
            part = sb("part", [P, 4, TILES, H + 1])
            rstd = sb("rstd", [P, TILES, 1])
            mult = sb("mult", [P, TILES, 1])
            zt = sb("zt", [T, NPAD], I32)
            zhot = zt[:].bitcast(F32)
            etab = sb("etab", [T, 2 * G])
            embT = sb("embT", [G, T])
            adT = sb("adT", [G, G])
            zz = sb("zz", [P, TILES, 2 * G])
            x0s = zz[:].rearrange("p t c -> p (t c)")[:, 0:TILES * H].rearrange("p (t c) -> p t c", c=H)
            drow = sb("drow", [P, TILES, DW])
            src_i = sb("src_i", [P, CHUNKS], I32)
            dst_i = sb("dst_i", [P, CHUNKS], I32)
            dis = sb("dis", [P, CHUNKS])
            cut = sb("cut", [P, CHUNKS])
            act_in = sb("act_in", [P, CHUNKS])
            zero = sb("zero", [P, (ROWS // P) * W])
            w1s = sb("w1s", [R, H])
            b1s = sb("b1s", [H, 1])
            w2s = sb("w2s", [H + 1, H])
            attr_sb = sb("attr_sb", [R, 4 * P])
            hid = sb("hid", [H + 1, 4 * P])
            gi_d = sb("gi_d", [P, 4], I32)
            gi_s = sb("gi_s", [P, 4], I32)
            seg = sb("seg", [P, 4])
            dg = sb("dg", [P, 4, DW])
            sg = sb("sg", [P, 4, G])
            same = sb("same", [P, 4, P])
            before = sb("before", [P, 4, P])
            nbef = sb("nbef", [P, 4])
            away = sb("away", [P, 4])
            sidx = sb("sidx", [P, 4], I32)
            hmc = sb("hmc", [P, 4, H])
            ad = sb("ad", [P, 4, G])
            ads = sb("ads", [P, 4, 1])
            gate_a = sb("gate_a", [P, 4, H])
            msg = sb("msg", [P, 4, H + 1])
            outrow = sb("outrow", [P, 4, W])
            ps_seg = pb("ps_seg", [P, 4, P])
            ps_h = pb("ps_h", [P, 512])
            ps_gate = pb("ps_gate", [P, 4, H])
            ps_sum = pb("ps_sum", [P, 4, H + 1])
            ps_z = pb("ps_z", [P, 7, 2 * G])
            ps_e = pb("ps_e", [P, 512])

            block = st.enter_context(nc.Block())

            @block.sync
            def _(sp):
                sp.dma_start(xs[:], tiles(x)).then_inc(s_load, 16)
                sp.dma_start(mult[:, :, 0], mult_n).then_inc(s_load, 16)
                sp.dma_start(gam[:], gamma.partition_broadcast(P)).then_inc(s_load, 16)
                sp.dma_start(bet[:], beta.partition_broadcast(P)).then_inc(s_load, 16)
                sp.dma_start(zt[:], types.partition_broadcast(T)).then_inc(s_load, 16)
                sp.dma_start(embT[:], emb_t).then_inc(s_load, 16)
                sp.dma_start(adT[:], adapt_t).then_inc(s_load, 16)
                sp.dma_start(etab[:, 0:G], emb).then_inc(s_load, 16)
                sp.dma_start(src_i[:], src).then_inc(s_load, 16)
                sp.dma_start(dst_i[:], dst).then_inc(s_load, 16)
                sp.dma_start(dis[:], dist).then_inc(s_load, 16)
                sp.dma_start(w1s[:], w1t).then_inc(s_load, 16)
                sp.dma_start(b1s[:], b1).then_inc(s_load, 16)
                sp.dma_start(w2s[:], w2e).then_inc(s_load, 16)
                sp.wait_ge(s_rows, 2)
                sp.dma_start(tiles(by_dst[:, :]), drow[:]).then_inc(s_tab, 16)
                sp.dma_start(tiles(by_src[:, :]), zz[:, :, 0:G]).then_inc(s_tab, 16)
                sp.dma_start(tiles(u_tab[:, :]), tmp[:]).then_inc(s_tab, 16)
                with sp.Fori(0, QUADS) as q:
                    sp.wait_ge(a_idx, q + 1)
                    sp.dma_start(attr_sb[:], attr_t[:, bass.ds(q * (4 * P), 4 * P)]).then_inc(a_at, 16)
                sp.wait_ge(s_add, 64 * (QUADS + 1))
                for r in range(4):
                    sp.dma_start(part[:, r], tiles(sums[r][0:NPAD, 0:H + 1])).then_inc(s_back, 16)
            @block.gpsimd
            def _(pool):
                pool.iota(pidx[:], [[0, 1]], base=0, channel_multiplier=1).then_inc(s_const, 1)
                pool.memset(ident[:], 0.0).then_inc(s_const, 1)
                pool.memset(tri[:], 1.0).then_inc(s_const, 1)
                pool.wait_ge(s_const, 3)
                pool.affine_select(out=ident[:], in_=ident[:], compare_op=ALU.not_equal, fill=1.0, base=0,
                                   pattern=[[-1, P]], channel_multiplier=1).then_inc(s_const, 1)
                pool.affine_select(out=tri[:], in_=tri[:], compare_op=ALU.is_gt, fill=0.0, base=0,
                                   pattern=[[-1, P]], channel_multiplier=1).then_inc(s_const, 1)

                pool.wait_ge(s_zero, 1)
                zero_sums(pool, zero, s_add)
                pool.wait_ge(s_tab, 48)
                with pool.Fori(0, QUADS) as q:
                    pool.wait_ge(a_idx, q + 1)
                    pool.sem_inc(s_mark, 1)
                    for c in range(4):
                        pool.indirect_dma_start(dg[:, c, :], None, by_dst[:, :],
                                                bass.IndirectOffsetOnAxis(ap=gi_d[:, c:c + 1], axis=0)).then_inc(a_gath, 16)
                        pool.indirect_dma_start(sg[:, c, :], None, by_src[:, :],
                                                bass.IndirectOffsetOnAxis(ap=gi_s[:, c:c + 1], axis=0)).then_inc(a_gath, 16)
                    pool.wait_ge(a_out, q + 1)
                    pool.sem_inc(s_mark, 1)
                    for c in range(4):
                        pool.indirect_dma_start(sums[c][:, :], bass.IndirectOffsetOnAxis(ap=sidx[:, c:c + 1], axis=0),
                                                outrow[:, c, :], None, compute_op=ALU.add).then_inc(s_add, 16)
            @block.scalar
            def _(act):
                act.wait_ge(s_ang, 1)
                nc.scalar.activation(act_in[:], dis[:], ACT.Sin).then_inc(s_sin, 1)
                act.wait_ge(s_var, 1)
                nc.scalar.activation(rstd[:], row2[:], ACT.Sqrt, bias=eps[:]).then_inc(s_sqrt, 1)
                with act.Fori(0, QUADS) as q:
                    act.wait_ge(a_h, q + 1)
                    nc.scalar.activation(hid[0:H, :], ps_h[0:H, :], ACT.Silu, bias=b1s[:]).then_inc(a_hid, 1)
                    act.wait_ge(a_sum, q + 1)
                    nc.scalar.activation(outrow[:, :, 0:H + 1], ps_sum[:], ACT.Copy).then_inc(a_out, 1)
                for k in range(2):
                    act.wait_ge(s_var, 2 + k)
                    nc.scalar.activation(rstd[:], row2[:], ACT.Sqrt, bias=eps[:]).then_inc(s_sqrt, 1)
            @block.tensor
            def _(pe):
                pe.wait_ge(s_load, 16 * len(loads))
                pe.wait_ge(s_const, 5)
                nc.tensor.matmul(ps_e[0:T, 0:G], embT[:], adT[:], start=True, stop=True).then_inc(s_e2, 1)
                pe.wait_ge(s_e2c, 1)
                for k in range(TILES // 7):
                    if k:
                        pe.wait_ge(s_zc, k)
                    for j in range(7):
                        t = 7 * k + j
                        last = nc.tensor.matmul(ps_z[:, j, :], zhot[:, t * P:(t + 1) * P], etab[:], start=True, stop=True)
                    last.then_inc(s_z, 1)

                with pe.Fori(0, QUADS) as q:
                    ids_across(pe, ps_seg, seg, a_idx, q + 1, a_seg)
                    pe.wait_ge(a_at, 16 * q + 16)
                    pe.sem_inc(s_turn, 1)
                    nc.tensor.matmul(ps_h[0:H, :], w1s[:], attr_sb[:], start=True, stop=True).then_inc(a_h, 1)
                    pe.wait_ge(a_hid, q + 1)
                    for c in range(4):
                        last = nc.tensor.matmul(ps_gate[:, c, :], hid[:, c * P:(c + 1) * P], w2s[:], start=True, stop=True)
                    last.then_inc(a_gate, 1)
                    pe.wait_ge(a_msg, q + 1)
                    for c in range(4):
                        last = nc.tensor.matmul(ps_sum[:, c, :], same[:, c, :], msg[:, c, :], start=True, stop=True)
                    last.then_inc(a_sum, 1)
            @block.vector
            def _(dve):
                V = nc.vector
                link = lambda ins: dve_link(dve, ins)

                nv = [0]

                def layernorm_relu(dst_ap, scale_shift=None):
                    link(V.tensor_reduce(row[:, :, 0], tmp[:], AX.X, ALU.add))
                    link(V.tensor_scalar(row[:], row[:], 1.0 / H, None, ALU.mult))
                    link(V.tensor_tensor(dst_ap, tmp[:], row[:].to_broadcast([P, TILES, H]), ALU.subtract))
                    link(V.tensor_tensor(tmp[:], dst_ap, dst_ap, ALU.mult))
                    link(V.tensor_reduce(row[:, :, 0], tmp[:], AX.X, ALU.add))
                    nv[0] += 1
                    V.tensor_scalar(row2[:], row[:], 1.0 / H, None, ALU.mult).then_inc(s_var, 1)
                    dve.wait_ge(s_sqrt, nv[0])
                    link(V.reciprocal(row2[:], rstd[:]))
                    link(V.tensor_tensor(dst_ap, dst_ap, row2[:].to_broadcast([P, TILES, H]), ALU.mult))
                    if scale_shift:
                        g_, b_ = scale_shift
                        link(V.tensor_tensor(dst_ap, dst_ap, g_[:].unsqueeze(1).to_broadcast([P, TILES, H]), ALU.mult))
                        link(V.tensor_tensor(dst_ap, dst_ap, b_[:].unsqueeze(1).to_broadcast([P, TILES, H]), ALU.add))
                    else:
                        link(V.tensor_scalar(dst_ap, dst_ap, 0.0, None, ALU.max))

                V.memset(zero[:], 0.0).then_inc(s_zero, 1)
                V.memset(eps[:], EPS)
                V.memset(hid[:], 1.0)
                V.memset(drow[:], 0.0)
                link(V.memset(outrow[:], 0.0))
                dve.wait_ge(s_load, 16 * len(loads))
                dve.wait_ge(s_const, 5)
                V.tensor_scalar(cut[:], dis[:], CUTOFF, 0.5, ALU.is_lt, ALU.mult)
                link(V.tensor_scalar(act_in[:], dis[:], CUTOFF, None, ALU.min))
                V.tensor_scalar(dis[:], act_in[:], -PI / CUTOFF, PI / 2, ALU.mult, ALU.add).then_inc(s_ang, 1)
                V.tensor_copy(src_f[:], src_i[:])
                V.tensor_copy(dst_f[:], dst_i[:])
                link(V.tensor_copy(pidx_f[:], pidx[:]))
                dve.wait_ge(s_sin, 1)
                link(V.tensor_scalar(act_in[:], act_in[:], 1.0, None, ALU.add))
                link(V.tensor_tensor(cut[:], cut[:], act_in[:], ALU.mult))
                for c in range(4):
                    link(V.tensor_scalar(dump[:, c:c + 1], pidx_f[:], float(DUMP), None, ALU.add))
                link(V.tensor_scalar(zhot, zt[:], float(T - 1), None, ALU.min))
                link(V.tensor_scalar(zhot, zhot, pidx_f[0:T, :], None, ALU.is_equal))
                dve.wait_ge(s_e2, 1)
                V.tensor_copy(etab[:, G:2 * G], ps_e[0:T, 0:G]).then_inc(s_e2c, 1)
                link(V.tensor_copy(tmp[:], xs[:]))
                layernorm_relu(hs_n[:])
                V.tensor_tensor(drow[:, :, 0:H], hs_n[:], mult[:].to_broadcast([P, TILES, H]), ALU.mult)
                V.tensor_copy(drow[:, :, H + G:H + G + 1], mult[:])
                for k in range(TILES // 7):
                    dve.wait_ge(s_z, k + 1)
                    V.tensor_copy(zz[:, 7 * k:7 * k + 7, :], ps_z[:]).then_inc(s_zc, 1)
                dve.wait_ge(s_zc, TILES // 7)
                V.tensor_copy(drow[:, :, H:H + G], zz[:, :, G:2 * G]).then_inc(s_rows, 1)
                V.memset(tmp[:], 1.0).then_inc(s_rows, 1)

                bufs = (gi_s, gi_d, seg, same, before, nbef, away, sidx, ps_seg)
                with dve.Fori(0, QUADS) as q:
                    col = dve.snap(q * 4)
                    gather_ids(dve, bufs, s_add, q * 64 + 64, col, True, src_f, a_idx)
                    merge(dve, bufs, a_seg, q, a_dve, q * 7, a_idx, None)
                    dve.wait_ge(a_gath, q * 128 + 128)
                    V.tensor_tensor(hmc[:], dg[:, :, 0:H], cut[:, bass.ds(col, 4)].unsqueeze(2).to_broadcast([P, 4, H]), ALU.mult)
                    V.tensor_copy(msg[:, :, H:H + 1], dg[:, :, H + G:H + G + 1])
                    V.tensor_tensor(ad[:], sg[:], dg[:, :, H:H + G], ALU.mult).then_inc(a_dve, 1)
                    dve.wait_ge(a_dve, q * 7 + 6)
                    V.tensor_reduce(ads[:, :, 0], ad[:], AX.X, ALU.add).then_inc(a_dve, 1)
                    dve.wait_ge(a_dve, q * 7 + 7)
                    dve.wait_ge(a_gate, q + 1)
                    V.tensor_tensor(gate_a[:], ps_gate[:], ads[:].to_broadcast([P, 4, H]), ALU.add).then_inc(a_mg, 1)
                    dve.wait_ge(a_mg, q + 1)
                    V.tensor_tensor(msg[:, :, 0:H], gate_a[:], hmc[:], ALU.mult).then_inc(a_msg, 1)

                dve.wait_ge(s_back, 64)
                link(V.tensor_tensor(part[:, 0], part[:, 0], part[:, 1], ALU.add))
                link(V.tensor_tensor(part[:, 2], part[:, 2], part[:, 3], ALU.add))
                link(V.tensor_tensor(part[:, 0], part[:, 0], part[:, 2], ALU.add))
                link(V.tensor_scalar(row[:], part[:, 0, :, H:H + 1], 1e-8, None, ALU.max))
                link(V.reciprocal(row2[:], row[:]))
                link(V.tensor_tensor(tmp[:], part[:, 0, :, 0:H], row2[:].to_broadcast([P, TILES, H]), ALU.mult))
                link(V.tensor_tensor(tmp[:], tmp[:], hs_n[:], ALU.add))
                layernorm_relu(acc[:], (gam, bet))
                link(V.tensor_tensor(xs[:], xs[:], acc[:], ALU.add))
                link(V.tensor_copy(tmp[:], xs[:]))
                layernorm_relu(hs_n[:])

        with ExitStack() as st:
            stage[0] = st
            first_f = sb("first_f", [P, ROWS_E])
            first_i = sb("first_i", [P, ROWS_E], I32)
            junk = sb("junk", [P, ROWS_E], F16)
            gstart = sb("gstart", [P, GT], I32)
            gstart_f = sb("gstart_f", [P, GT])
            gcol0 = sb("gcol0", [P, GT])
            grow = sb("grow", [P, GT])
            widx = sb("widx", [P, GT, WROWS], I32)
            jrow = sb("jrow", [P, WROWS])
            NW = GT * WROWS * RE
            win = first_i[:, 0:2 * NW].rearrange("p (t j e) -> p t j e", t=GT, j=WROWS)
            low_i = first_f[:, 0:NW].bitcast(I32).rearrange("p (t j e) -> p t j e", t=GT, j=WROWS)
            tile_i = first_f[:, NW:2 * NW].bitcast(I32).rearrange("p (t j e) -> p t j e", t=GT, j=WROWS)
            low = sb("low", [P, GT, WROWS * RE])
            key = sb("key", [P, GT, WROWS * RE])
            e_low = sb("e_low", [P, WCH, GT * P])
            e_key = sb("e_key", [P, WCH, GT * P])
            cols_i = sb("cols_i", [P, GCOLS], I32)
            cols = sb("cols", [P, GCOLS], F16)
            TURN, DEPTH = 2, 4
            hot_low = sb("hot_low", [P, DEPTH, TURN * WCH, P], F16)
            hot_key = sb("hot_key", [P, DEPTH, TURN * WCH, GCOLS], F16)
            full = sb("full", [P, 2, TILES, P], F8)
            one16 = sb("one16", [P, 1], F16)
            onesf = sb("onesf", [P, P])
            over = sb("over", [P, TILES])
            over2 = sb("over2", [P, 2])
            spare = junk[:, 0:NPAD]
            minus = sb("minus", [P, 1])
            check2 = sb("check2", [P, 2])
            ok2 = sb("ok2", [1, 2])
            banks = [pb(f"counts{k}", [P, 512]) for k in range(2 * TURN)]
            ps_tr = [pb(f"ps_tr{k}", [P, 4, P]) for k in range(2)]
            ps_deg = pb("ps_deg", [P, 1])
            ps_ok = pb("ps_ok", [P, 2])
            TURNS = GPB // TURN
            NTR = GT * WCH * 2
            block = st.enter_context(nc.Block())

            def blocks(engine, body):
                body(0, 0, True)
                with engine.Fori(0, (TILES - 1) // 2) as k:
                    b = engine.snap(k * 2 + 1)
                    body(b, 1, False)
                    body(b + 1, 0, False)

            @block.sync
            def _(sp):
                sp.dma_start(first_i[:], dst_first.partition_broadcast(P)).then_inc(c_load, 16)

                sp.sem_inc(c_free, 1)

                def store(b, slot, first):
                    sp.wait_ge(c_took, b * TURNS + TURNS)
                    sp.sem_inc(s_go, 1)
                    sp.dma_start(counts_d[bass.ds(b, 1) if not first else slice(0, 1)].rearrange("b p c -> p (b c)"),
                                 full[:, slot].rearrange("p t c -> p (t c)").bitcast(U8)).then_inc(c_stored[slot], 16)
                    sp.wait_ge(c_stored[slot], b * 8 + (8 if slot else 16))
                    sp.sem_inc(c_free, 1)
                blocks(sp, store)
                sp.wait_ge(c_stored[0], 16 * (TILES // 2 + 1))
                sp.wait_ge(c_stored[1], 16 * (TILES // 2))

            @block.gpsimd
            def _(pool):
                pool.iota(gstart[:], [[P * GD, GT]], base=0, channel_multiplier=GD).then_inc(c_io, 1)
                pool.iota(cols_i[:], [[1, GCOLS]], base=0, channel_multiplier=0).then_inc(c_io, 1)
                pool.iota(widx[:, 0, :], [[1, WROWS]], base=0, channel_multiplier=0).then_inc(c_io, 1)
                pool.wait_ge(c_idx, 1)
                for t in range(GT):
                    for j in range(WROWS):
                        pool.indirect_dma_start(win[:, t, j, :], None, edge_rows,
                                                bass.IndirectOffsetOnAxis(ap=widx[:, t, j:j + 1], axis=0)).then_inc(c_win, 16)

            @block.tensor
            def _(pe):
                pe.wait_ge(c_key, 1)
                n = 0
                for k in range(NTR // 3):
                    if k >= 2:
                        pe.wait_ge(c_trc, k - 1)
                    for j in range(3):
                        arr, t = divmod(n // WCH, GT)
                        c = n % WCH
                        last = nc.tensor.transpose(ps_tr[k % 2][:, j, :], (low, key)[arr][:, t, c * P:(c + 1) * P], ident[:])
                        n += 1
                    last.then_inc(c_tr, 1)

                def degrees(b, slot):
                    pe.wait_ge(c_took, b * TURNS + TURNS)
                    pe.sem_inc(c_turn, 1)
                    for t in range(TILES):
                        last = nc.tensor.matmul(ps_deg[:], full[:, slot, t, :], one16[:], start=(t == 0), stop=(t == TILES - 1))
                    last.then_inc(c_deg, 1)

                def count_block(b, slot, first):
                    for turn in range(TURNS):
                        n = b * TURNS + turn
                        pe.wait_ge(c_one, n + 1)
                        if not (first and turn < 2):
                            pe.wait_ge(c_took, n - 1)
                        for g in range(TURN):
                            for c in range(WCH):
                                k = g * WCH + c
                                last = nc.tensor.matmul(banks[(turn % 2) * TURN + g][:, 0:GCOLS], hot_low[:, turn % DEPTH, k, :],
                                                        hot_key[:, turn % DEPTH, k, :], start=(c == 0), stop=(c == WCH - 1))
                        last.then_inc(c_cnt, 1)
                        if turn == 1 and not first:
                            degrees(b - 1, 1 - slot)
                blocks(pe, count_block)
                degrees(TILES - 1, 0)
                pe.wait_ge(c_dve, 1)
                nc.tensor.matmul(ps_ok[:], onesf[:], check2[:], start=True, stop=True).then_inc(c_sum, 1)

            @block.scalar
            def _(act):
                def take_block(b, slot, first):
                    for turn in range(TURNS):
                        n = b * TURNS + turn
                        act.wait_ge(c_cnt, n + 1)
                        if turn == 0 and not first:
                            wait_slot(act, b, slot)
                        act.sem_inc(c_mark, 1)
                        for g in range(TURN):
                            j = turn * TURN + g
                            bank = banks[(turn % 2) * TURN + g][:, 0:GCOLS]
                            last = nc.scalar.activation(full[:, slot, :, GD * j:GD * j + GD], bank.rearrange("p (d s) -> p s d", d=GD),
                                                        ACT.Copy, saturate=False)
                        last.then_inc(c_took, 1)
                        if turn == 2 and not first:
                            act.wait_ge(c_deg, b)
                            excess(b - 1, 1 - slot)
                            nc.scalar.activation(deg[:, bass.ds(b - 1, 1), :].rearrange("p a b -> p (a b)"), ps_deg[:], ACT.Copy).then_inc(c_degc, 1)

                def excess(b, slot):
                    act.wait_ge(c_took, b * TURNS + TURNS)
                    act.sem_inc(c_mark, 1)
                    nc.scalar.activation(spare, full[:, slot].rearrange("p t c -> p (t c)"), ACT.Relu, bias=minus[:],
                                         accum_out=over2[:, slot:slot + 1]).then_inc(c_over, 1)
                    act.wait_ge(c_over, b + 1)
                    nc.scalar.activation(over[:, bass.ds(b, 1)] if not isinstance(b, int) else over[:, b:b + 1],
                                         over2[:, slot:slot + 1], ACT.Copy).then_inc(c_over2, 1)

                def wait_slot(act, b, slot):
                    act.wait_ge(c_free, b)

                act.wait_ge(c_io, 4)
                blocks(act, take_block)
                act.wait_ge(c_deg, TILES)
                excess(TILES - 1, 0)
                nc.scalar.activation(deg[:, TILES - 1, :], ps_deg[:], ACT.Copy).then_inc(c_degc, 1)

            @block.vector
            def _(dve):
                V = nc.vector
                link = lambda ins: dve_link(dve, ins)
                dve.wait_ge(c_io, 3)
                V.memset(minus[:], -float(EXACT))
                V.memset(one16[:], 1.0)
                V.memset(onesf[:], 1.0)
                V.memset(over[:], 0.0).then_inc(c_io, 1)
                V.tensor_copy(cols[:], cols_i[:])
                V.tensor_copy(jrow[:], widx[:, 0, :])
                link(V.tensor_copy(gstart_f[:], gstart[:]))
                dve.wait_ge(c_load, 16)
                link(V.tensor_copy(first_f[:], first_i[:]))
                for t in range(GT):
                    link(V.tensor_scalar(junk[:], first_f[:], gstart_f[:, t:t + 1], None, ALU.is_lt, ALU.add,
                                         accum_out=grow[:, t:t + 1]))
                link(V.tensor_scalar(grow[:], grow[:], -1.0, 0.0, ALU.add, ALU.max))
                V.tensor_tensor(widx[:], jrow[:].unsqueeze(1).to_broadcast([P, GT, WROWS]),
                                grow[:].unsqueeze(2).to_broadcast([P, GT, WROWS]), ALU.add).then_inc(c_idx, 1)
                dve.wait_ge(c_win, 16 * GT * WROWS)
                w = win.rearrange("p t j e -> p (t j) e")
                V.tensor_scalar(low_i.rearrange("p t j e -> p (t j) e"), w[:, :, 0:RE], P - 1, None, ALU.bitwise_and)
                link(V.tensor_scalar(tile_i.rearrange("p t j e -> p (t j) e"), w[:, :, 0:RE], 7, None, ALU.logical_shift_right))
                V.tensor_copy(low[:], low_i.rearrange("p t j e -> p t (j e)"))
                link(V.scalar_tensor_tensor(key[:].rearrange("p t (j e) -> p (t j) e", e=RE), w[:, :, RE:2 * RE], float(TILES),
                                            tile_i.rearrange("p t j e -> p (t j) e"), ALU.mult, ALU.add))
                link(V.tensor_scalar(gcol0[:], gstart_f[:], float(TILES), None, ALU.mult))
                V.tensor_tensor(key[:], key[:], gcol0[:].unsqueeze(2).to_broadcast([P, GT, WROWS * RE]), ALU.subtract).then_inc(c_key, 1)
                n = 0
                for k in range(NTR // 3):
                    dve.wait_ge(c_tr, k + 1)
                    arr, t = divmod(n // WCH, GT)
                    V.tensor_copy((e_low, e_key)[arr][:, :, t * P:(t + 1) * P], ps_tr[k % 2][:, 0:WCH, :]).then_inc(c_trc, 1)
                    n += WCH
                dve.wait_ge(c_trc, NTR // 3)

                def hot_block(b, slot, first):
                    for turn in range(TURNS):
                        n = b * TURNS + turn
                        if not (first and turn < DEPTH):
                            dve.wait_ge(c_cnt, n - DEPTH + 1)
                        for g in range(TURN):
                            col = dve.snap(b * GPB + (turn * TURN + g)) if not first else turn * TURN + g
                            for c in range(WCH):
                                k = g * WCH + c
                                at = bass.ds(col, 1) if not first else slice(col, col + 1)
                                V.tensor_scalar(hot_key[:, turn % DEPTH, k, :], cols[:], e_key[:, c, at], None, ALU.is_equal)
                                last = V.tensor_scalar(hot_low[:, turn % DEPTH, k, :], cols[:, 0:P], e_low[:, c, at], None, ALU.is_equal)
                        last.then_inc(c_one, 1)
                blocks(dve, hot_block)
                dve.wait_ge(c_degc, TILES)
                dve.wait_ge(c_over2, TILES)
                V.tensor_reduce(check2[:, 0:1], deg[:, :, 0], AX.X, ALU.add)
                V.tensor_reduce(check2[:, 1:2], over[:], AX.X, ALU.add).then_inc(c_dve, 1)
                dve.wait_ge(c_sum, 1)
                V.tensor_scalar(ok2[:, 0:1], ps_ok[0:1, 0:1], float(EPAD), None, ALU.is_equal)
                link(V.tensor_scalar(ok2[:, 1:2], ps_ok[0:1, 1:2], 0.0, None, ALU.is_equal))
                link(V.tensor_tensor(dense[:], ok2[:, 0:1], ok2[:, 1:2], ALU.mult))

        with ExitStack() as st:
            stage[0] = st
            x0s = sb("x0s1", [P, TILES, H])
            acc = sb("acc1", [P, TILES, H])

            ring = sb("ring", [P, RING, TILES * P], F8)
            u_hl = sb("u_hl", [P, 2, TILES, 2 * H], F16)
            low_sum = sb("low_sum", [P, 2, 4, H])
            t_sb = sb("t_sb", [P, 4, H])
            ps_u = [pb(f"ps_u{k}", [P, 4, 2 * H]) for k in range(2)]

            part = sb("part1", [P, 4, TILES, H])
            zero = sb("zero1", [P, (ROWS // P) * W])
            gi_s = sb("gi_s1", [P, 4], I32)
            seg = sb("seg1", [P, 4])
            ug = sb("ug", [P, 4, H])
            same = sb("same1", [P, 4, P])
            before = sb("before1", [P, 4, P])
            nbef = sb("nbef1", [P, 4])
            away = sb("away1", [P, 4])
            sidx = sb("sidx1", [P, 4], I32)
            outrow = sb("outrow1", [P, 4, W])
            ps_seg = pb("ps_seg1", [P, 4, P])
            ps_sum = pb("ps_sum1", [P, 4, H + 1])
            bufs = (gi_s, None, seg, same, before, nbef, away, sidx, ps_seg)
            L1PASSES = STEPS + 1
            ROUNDS = TILES // RING
            PARTS = ((0, 4), (4, 3))
            block = st.enter_context(nc.Block())

            def either(engine, if_dense, if_not):
                way = engine.value_load(dense[:], min_val=0, max_val=1)
                with engine.If(way > 0):
                    if_dense()
                with engine.If(way < 1):
                    if_not()

            @block.sync
            def _(sp):
                def with_matrix():
                    def load_round(it, r, first):
                        for j in range(RING):
                            if not first:
                                sp.wait_ge(d_free, r * RING + (it * TILES - RING + 1 + j))
                                sp.sem_inc(s_go, 1)
                            at = slice(j, j + 1) if first else bass.ds(r * RING + j, 1)
                            sp.dma_start(ring[:, j, :].bitcast(U8), counts_d[at].rearrange("b p c -> p (b c)")).then_inc(d_in[j], 16)
                    load_round(0, 0, True)
                    for it in range(STEPS):
                        with sp.Fori(0 if it else 1, ROUNDS) as r:
                            load_round(it, r, False)

                def over_edges():
                    for p in range(L1PASSES):
                        sp.wait_ge(b_add[p], 64 * (QUADS + 1))
                        for r in range(4):
                            sp.dma_start(part[:, r], tiles(sums[r][0:NPAD, 0:H])).then_inc(b_back, 16)
                        sp.wait_ge(b_used, p + 1)
                        sp.dma_start(tiles(u_tab[:, :]), acc[:]).then_inc(b_u, 16)
                    sp.wait_ge(b_u, 16 * L1PASSES)

                either(sp, with_matrix, over_edges)
                sp.wait_ge(s_fin, 1)
                sp.dma_start(tiles(out), xs[:]).then_inc(s_outd, 16)
                sp.wait_ge(s_outd, 16)

            @block.gpsimd
            def _(pool):
                def over_edges():
                    pool.wait_ge(s_zero, 2)
                    for p in range(L1PASSES):
                        zero_sums(pool, zero, b_add[p])
                        with pool.Fori(0, QUADS) as q:
                            n = q + p * QUADS
                            pool.wait_ge(b_idx, n + 1)
                            pool.sem_inc(s_mark, 1)
                            for c in range(4):
                                pool.indirect_dma_start(ug[:, c, :], None, u_tab[:, :],
                                                        bass.IndirectOffsetOnAxis(ap=gi_s[:, c:c + 1], axis=0)).then_inc(b_gath[p], 16)
                            pool.wait_ge(b_out, n + 1)
                            pool.sem_inc(s_mark, 1)
                            for c in range(4):
                                pool.indirect_dma_start(sums[c][:, :], bass.IndirectOffsetOnAxis(ap=sidx[:, c:c + 1], axis=0),
                                                        outrow[:, c, :], None, compute_op=ALU.add).then_inc(b_add[p], 16)
                        pool.wait_ge(b_u, (p + 1) * 16)

                either(pool, lambda: pool.sem_inc(s_mark, 1), over_edges)

            @block.scalar
            def _(act):
                def with_matrix():
                    act.wait_ge(d_sq, 1)
                    nc.scalar.activation(dinv[:], deg[:], ACT.Sqrt).then_inc(d_ac, 1)
                    with act.Fori(0, STEPS * ROUNDS) as n:
                        for k, (j0, nj) in enumerate(PARTS):
                            act.wait_ge(d_sum[k], n + 1)
                            nc.scalar.activation(low_sum[:, k, 0:nj, :], ps_u[k][:, 0:nj, H:2 * H], ACT.Copy).then_inc(d_lo[k], 1)

                def over_edges():
                    with act.Fori(0, QUADS) as q:
                        act.wait_ge(b_sum, q + 1)
                        nc.scalar.activation(outrow[:, :, 0:H], ps_sum[:, :, 0:H], ACT.Copy).then_inc(b_out, 1)
                    act.wait_ge(d_sq, 1)
                    nc.scalar.activation(dinv[:], deg[:], ACT.Sqrt).then_inc(d_ac, 1)
                    with act.Fori(QUADS, L1PASSES * QUADS) as n:
                        act.wait_ge(b_sum, n + 1)
                        nc.scalar.activation(outrow[:, :, 0:H], ps_sum[:, :, 0:H], ACT.Copy).then_inc(b_out, 1)

                either(act, with_matrix, over_edges)

            @block.tensor
            def _(pe):
                def with_matrix():
                    for it in range(STEPS):
                        pe.wait_ge(d_u, it + 1)
                        with pe.Fori(0, ROUNDS) as r:
                            n = r + it * ROUNDS
                            for k, (j0, nj) in enumerate(PARTS):
                                pe.wait_ge(d_bank[k], n + 1)
                                for j in range(j0, j0 + nj):
                                    pe.wait_ge(d_in[j], n * 16 + 16)
                                    pe.sem_inc(d_turn, 1)
                                    for t in range(TILES):
                                        last = nc.tensor.matmul(ps_u[k][:, j - j0, :], ring[:, j, t * P:(t + 1) * P],
                                                                u_hl[:, it % 2, t, :], start=(t == 0), stop=(t == TILES - 1))
                                    last.then_inc(d_free, 1)
                                pe.wait_ge(d_free, n * RING + (j0 + nj))
                                pe.sem_inc(d_sum[k], 1)

                def over_edges():
                    for p in range(L1PASSES):
                        with pe.Fori(0, QUADS) as q:
                            n = q + p * QUADS
                            ids_across(pe, ps_seg, seg, b_idx, n + 1, b_seg)
                            pe.wait_ge(b_eq, n + 1)
                            pe.wait_ge(b_gath[p], 64 * q + 64)
                            for c in range(4):
                                last = nc.tensor.matmul(ps_sum[:, c, 0:H], same[:, c, :], ug[:, c, :], start=True, stop=True)
                            last.then_inc(b_sum, 1)

                either(pe, with_matrix, over_edges)

            @block.vector
            def _(dve):
                V = nc.vector
                link = lambda ins: dve_link(dve, ins)
                V.memset(zero[:], 0.0).then_inc(s_zero, 1)
                link(V.memset(outrow[:], 0.0))
                linked = count[0]

                def start(scale):
                    link(V.tensor_scalar(deg[:], deg[:], 1.0, None, ALU.add))
                    link(V.reciprocal(fifth[:], deg[:]))
                    link(V.tensor_scalar(fifth[:], fifth[:], 1.0 - ALPHA, None, ALU.mult))
                    dve.sem_inc(d_sq, 1)
                    dve.wait_ge(d_ac, 1)
                    link(V.reciprocal(row[:], dinv[:]))
                    link(V.tensor_copy(dinv[:], row[:]))
                    link(V.tensor_scalar(row[:], row[:], scale, None, ALU.mult))
                    link(V.tensor_tensor(acc[:], hs_n[:], row[:].to_broadcast([P, TILES, H]), ALU.mult))

                def finish(scale):
                    link(V.tensor_tensor(row[:], deg[:], dinv[:], ALU.mult))
                    link(V.tensor_scalar(row[:], row[:], 1.0 / scale, None, ALU.mult))
                    link(V.tensor_tensor(acc[:], acc[:], row[:].to_broadcast([P, TILES, H]), ALU.mult))
                    V.tensor_tensor(xs[:], xs[:], acc[:], ALU.add).then_inc(s_fin, 1)

                def with_matrix():
                    start(SCALE)
                    link(V.tensor_scalar(x0s[:], acc[:], ALPHA, None, ALU.mult))
                    link(V.tensor_copy(u_hl[:, 0, :, 0:H], acc[:]))
                    V.tensor_tensor(u_hl[:, 0, :, H:2 * H], acc[:], u_hl[:, 0, :, 0:H], ALU.subtract).then_inc(d_u, 1)
                    for k in range(2):
                        dve.sem_inc(d_bank[k], 1)
                    for it in range(STEPS):
                        with dve.Fori(0, ROUNDS) as r:
                            n = r + it * ROUNDS
                            for k, (j0, nj) in enumerate(PARTS):
                                c0 = (n * 2 + k) * 5
                                b = dve.snap(r * RING + j0)
                                own, t_ = acc[:, bass.ds(b, nj), :], t_sb[:, 0:nj, :]
                                hi, lo = (u_hl[:, (it + 1) % 2, bass.ds(b, nj), c * H:(c + 1) * H] for c in range(2))
                                dve.wait_ge(d_lo[k], n + 1)
                                V.tensor_tensor(t_, ps_u[k][:, 0:nj, 0:H], low_sum[:, k, 0:nj, :], ALU.add).then_inc(d_bank[k], 1)
                                dve.wait_ge(d_bank[k], n + 2)
                                V.tensor_tensor(t_, t_, own, ALU.add).then_inc(d_dve, 1)
                                dve.wait_ge(d_dve, c0 + 1)
                                V.tensor_tensor(t_, t_, fifth[:, bass.ds(b, nj), :].to_broadcast([P, nj, H]), ALU.mult).then_inc(d_dve, 1)
                                dve.wait_ge(d_dve, c0 + 2)
                                V.tensor_tensor(own, t_, x0s[:, bass.ds(b, nj), :], ALU.add).then_inc(d_dve, 1)
                                dve.wait_ge(d_dve, c0 + 3)
                                V.tensor_copy(hi, own).then_inc(d_dve, 1)
                                dve.wait_ge(d_dve, c0 + 4)
                                V.tensor_tensor(lo, own, hi, ALU.subtract).then_inc(d_dve, 1)
                        dve.wait_ge(d_dve, (it + 1) * ROUNDS * 10)
                        dve.sem_inc(d_u, 1)
                    finish(SCALE)

                def over_edges():
                    count[0] = linked

                    def edge_pass(p):
                        with dve.Fori(0, QUADS) as q:
                            n = q + p * QUADS
                            col = dve.snap(q * 4)
                            gather_ids(dve, bufs, b_add[p], q * 64 + 64, col, False, dst_f, b_idx)
                            merge(dve, bufs, b_seg, n, b_dve, n * 5, b_idx, b_eq)
                        dve.wait_ge(b_back, 64 * (p + 1))
                        link(V.tensor_tensor(part[:, 0], part[:, 0], part[:, 1], ALU.add))
                        link(V.tensor_tensor(part[:, 2], part[:, 2], part[:, 3], ALU.add))
                        link(V.tensor_tensor(part[:, 0], part[:, 0], part[:, 2], ALU.add))

                    edge_pass(0)
                    link(V.tensor_copy(deg[:], part[:, 0, :, 0:1]))
                    start(1.0)
                    V.tensor_scalar(x0s[:], acc[:], ALPHA, None, ALU.mult).then_inc(b_used, 1)
                    for p in range(1, L1PASSES):
                        edge_pass(p)
                        dve.wait_ge(b_u, 16 * p)
                        link(V.tensor_tensor(acc[:], acc[:], part[:, 0], ALU.add))
                        link(V.tensor_tensor(acc[:], acc[:], fifth[:].to_broadcast([P, TILES, H]), ALU.mult))
                        V.tensor_tensor(acc[:], acc[:], x0s[:], ALU.add).then_inc(b_used, 1)
                    dve.wait_ge(b_used, L1PASSES)
                    dve.wait_ge(b_u, 16 * L1PASSES)
                    finish(1.0)

                either(dve, with_matrix, over_edges)


def kernel(x, src, dst, edge_attr_40, edge_weight, node_type_119, node_vec, L0_gnn_W1, L0_gnn_b1, L0_gnn_W2,
           L0_gnn_b2, L0_gnn_emb, L0_gnn_adaptW, L0_gnn_gamma, L0_gnn_beta):
    import numpy as np
    import concourse.bacc as bacc
    from concourse.bass_utils import run_bass_kernel_spmd

    def padded(a, n, value=0):
        a = np.asarray(a)
        return np.concatenate([a, np.full((n - a.shape[0],) + a.shape[1:], value, a.dtype)])

    def by_chunk(a):
        return np.ascontiguousarray(a.reshape(CHUNKS, P).T)

    fill = np.arange(EPAD - E)
    src, dst = (np.concatenate([np.asarray(a), (N + f).astype(np.asarray(a).dtype)])
                for a, f in ((src, fill % (NPAD - N)), (dst, fill * (NPAD - N) // fill.size)))

    arrays = {
        "x": padded(x, NPAD),
        "src": by_chunk(src),
        "dst": by_chunk(dst),
        "dist": by_chunk(padded(edge_weight, EPAD, 2 * CUTOFF)),
        "attr_t": np.ascontiguousarray(padded(edge_attr_40, EPAD).T),
        "mult_n": np.ascontiguousarray(padded(node_vec, NPAD).reshape(TILES, P).T),
        "types": padded(node_type_119, NPAD),
        "w1t": np.ascontiguousarray(np.asarray(L0_gnn_W1).T),
        "b1": np.asarray(L0_gnn_b1).reshape(H, 1),
        "w2e": np.concatenate([np.asarray(L0_gnn_W2).T, np.asarray(L0_gnn_b2).reshape(1, H)]),
        "emb": np.asarray(L0_gnn_emb),
        "emb_t": np.ascontiguousarray(np.asarray(L0_gnn_emb).T),
        "adapt_t": np.ascontiguousarray(np.asarray(L0_gnn_adaptW).T),
        "gamma": np.asarray(L0_gnn_gamma),
        "beta": np.asarray(L0_gnn_beta),
        "edge_rows": np.concatenate([padded(src, EROWS * RE).reshape(EROWS, RE),
                                     padded(dst, EROWS * RE, 2 * NPAD).reshape(EROWS, RE)], axis=1),
        "dst_first": dst[::RE],
    }
    nc = bacc.Bacc("TRN2", target_bir_lowering=False, num_devices=1)
    maps = {f"in_{n}": np.ascontiguousarray(a) for n, a in arrays.items()}
    args = [nc.dram_tensor(f"in_{n}", a.shape, mybir.dt.from_np(a.dtype), kind="ExternalInput").ap() for n, a in arrays.items()]
    out = nc.dram_tensor("out_0", (NPAD, H), F32, kind="ExternalOutput").ap()
    gnn_kernel(nc, *args, out)
    r = run_bass_kernel_spmd(nc, [maps], core_ids=[0])
    return r.results[0]["out_0"][:N]
```

```python
from contextlib import ExitStack

import concourse.bass as bass
from concourse import mybir

F32, I32, F16 = mybir.dt.float32, mybir.dt.int32, mybir.dt.float16
ALU, ACT, AX = mybir.AluOpType, mybir.ActivationFunctionType, mybir.AxisListType

P = 128
N, H, R, G, T, E = 6250, 48, 40, 32, 119, 206250
TILES = -(-N // P)
NPAD = TILES * P
CHUNKS = 16 * -(-E // (16 * P))
EPAD = CHUNKS * P
QUADS = CHUNKS // 4
BATCH = 8
BATCHES = CHUNKS // BATCH
ROOM = 2 * P
PAIRS = BATCHES // 2
IDS = 3
DUMP = NPAD
ROWS = NPAD + P
W = 64
DW = 96
STEPS = 5
GD = 8
GCOLS = GD * TILES
GROUPS = NPAD // GD
GPB = P // GD
TURN, DEPTH = 2, 4
XP = GPB // TURN // 2
XC = NPAD // XP
FLIPS = -(-TILES // 4)
GT = -(-GROUPS // P)
RE = 32
WROWS = 12
WCH = WROWS * RE // P
ROWS_E = EPAD // RE
EROWS = ROWS_E + 16
EXACT = 15
SCALE = 4096.0
MULT_SCALE = 1024.0
MULT_MAX = 60.0
RING = 7
F8, U8 = mybir.dt.float8e4, mybir.dt.uint8
ALPHA = 0.8
CUTOFF = 6.0
EPS = 1e-5
PI = 3.141592653589793


def gnn_kernel(nc, x, src, dst, dist, attr, attr_t, mult_n, types, w1t, b1, w2e, emb, emb_t, adapt_t, gamma, beta,
               edge_rows, dst_first, out):
    ctx = ExitStack()
    with ctx:
        stage = [ctx]

        def sb(name, shape, dt=F32):
            return stage[0].enter_context(nc.sbuf_tensor(name, shape, dt))

        def pb(name, shape):
            return stage[0].enter_context(nc.psum_tensor(name, shape, F32))

        def sem(name):
            return ctx.enter_context(nc.semaphore(name))

        def tiles(ap):
            return ap.rearrange("(t p) c -> p t c", p=P)

        by_dst = nc.dram_tensor("by_dst", [NPAD, DW], F32, kind="Internal")
        by_src = nc.dram_tensor("by_src", [NPAD, G], F32, kind="Internal")
        u_tab = nc.dram_tensor("u_tab", [NPAD, H], F32, kind="Internal")
        sums = [nc.dram_tensor(f"sums{r}", [ROWS, W], F32, kind="Internal") for r in range(4)]
        counts_d = nc.dram_tensor("counts_d", [TILES, P, TILES * P], U8, kind="Internal")

        xs = sb("xs", [P, TILES, H])
        hs_n = sb("hs_n", [P, TILES, H])
        row = sb("row", [P, TILES, 1])
        row2 = sb("row2", [P, TILES, 1])
        deg = sb("deg", [P, TILES, 1])
        dinv = sb("dinv", [P, TILES, 1])
        fifth = sb("fifth", [P, TILES, 1])
        gam = sb("gam", [P, H])
        bet = sb("bet", [P, H])
        pidx = sb("pidx", [P, 1], I32)
        pidx_f = sb("pidx_f", [P, 1])
        dump = sb("dump", [P, 4])
        src_f = sb("src_f", [P, CHUNKS])
        dst_f = sb("dst_f", [P, CHUNKS])
        eps = sb("eps", [P, 1])
        ident = sb("ident", [P, P])
        tri = sb("tri", [P, P])
        cut = sb("cut", [P, CHUNKS])
        tot = sb("tot", [P, TILES, 1])
        dense_all = sb("dense_all", [P, 1])
        few_all = sb("few_all", [P, 1])
        dense = sb("dense", [1, 1], I32)
        few = sb("few", [1, 1], I32)

        loads = ["x", "mult", "gam", "bet", "zt", "embT", "adT", "emb", "src", "dst", "dis"]
        s_load = sem("s_load")
        s_const = sem("s_const")
        s_zero = sem("s_zero")
        s_var = sem("s_var")
        s_sqrt = sem("s_sqrt")
        s_ang = sem("s_ang")
        s_sin = sem("s_sin")
        s_e2 = sem("s_e2")
        s_e2c = sem("s_e2c")
        s_z = sem("s_z")
        s_zc = sem("s_zc")
        s_rows = sem("s_rows")
        s_tab = sem("s_tab")
        s_dve = sem("s_dve")
        a_idx, a_seg, a_at, a_h, a_hid, a_gate, a_gath, a_msg, a_sum, a_out, a_dve, a_mg = (
            sem("a_" + n) for n in ("idx", "seg", "at", "h", "hid", "gate", "gath", "msg", "sum", "out", "dve", "mg"))
        b_idx, b_seg, b_eq, b_sum, b_out, b_dve = (
            sem("b_" + n) for n in ("idx", "seg", "eq", "sum", "out", "dve"))
        b_gath = [sem(f"b_gath{p}") for p in range(STEPS + 1)]
        b_add = [sem(f"b_add{p}") for p in range(STEPS + 1)]
        s_add = sem("s_add")
        s_mark, s_turn, s_go = (sem("s_" + n) for n in ("mark", "turn", "go"))
        s_tot = sem("s_tot")
        s_ones = sem("s_ones")
        s_back = sem("s_back")
        b_back = sem("b_back")
        b_used = sem("b_used")
        b_u = sem("b_u")
        c_load, c_idx, c_win, c_key, c_tr, c_trc, c_dve, c_one, c_cnt, c_took, c_free, c_degc, c_sum = (
            sem("c_" + n) for n in ("load", "idx", "win", "key", "tr", "trc", "dve", "one", "cnt", "took", "free", "degc", "sum"))
        c_stored = [sem(f"c_stored{k}") for k in range(2)]
        c_over, c_over2 = sem("c_over"), sem("c_over2")
        c_turn, c_mark = sem("c_turn"), sem("c_mark")
        c_io = sem("c_io")
        d_in = [sem(f"d_in{j}") for j in range(RING)]
        d_lo, d_bank = ([sem(f"d_{n}{k}") for k in range(2)] for n in ("lo", "bank"))
        d_free, d_u, d_turn, d_dve, d_sq, d_ac = (sem("d_" + n) for n in ("free", "u", "turn", "dve", "sq", "ac"))
        s_fin = sem("s_fin")
        s_outd = sem("s_outd")
        r_keep, r_rank, r_io = (sem("r_" + n) for n in ("keep", "rank", "io"))
        p_hot, p_pay, p_tr, p_atc, p_pc = (sem("p_" + n) for n in ("hot", "pay", "tr", "atc", "pc"))
        p_gath = [sem(f"p_gath{b}") for b in range(2)]
        c_flip, c_flipc, c_tot = (sem("c_" + n) for n in ("flip", "flipc", "tot"))

        count = [0]
        variances = [0]
        TURNS = GPB // TURN
        TPP = TURNS // 2

        def at(i, n=1):
            return slice(i, i + n) if isinstance(i, int) else bass.ds(i, n)

        def either(engine, flag, if_so, if_not):
            way = engine.value_load(flag[:], min_val=0, max_val=1)
            with engine.If(way > 0):
                if_so()
            with engine.If(way < 1):
                if_not()

        def layernorm(dve, to, tmp, rstd, scale_shift=None):
            V = nc.vector
            link = lambda ins: dve_link(dve, ins)
            link(V.tensor_reduce(row[:, :, 0], tmp[:], AX.X, ALU.add))
            link(V.tensor_scalar(row[:], row[:], 1.0 / H, None, ALU.mult))
            link(V.tensor_tensor(to, tmp[:], row[:].to_broadcast([P, TILES, H]), ALU.subtract))
            link(V.tensor_tensor(tmp[:], to, to, ALU.mult))
            link(V.tensor_reduce(row[:, :, 0], tmp[:], AX.X, ALU.add))
            variances[0] += 1
            V.tensor_scalar(row2[:], row[:], 1.0 / H, None, ALU.mult).then_inc(s_var, 1)
            dve.wait_ge(s_sqrt, variances[0])
            link(V.reciprocal(row2[:], rstd[:]))
            link(V.tensor_tensor(to, to, row2[:].to_broadcast([P, TILES, H]), ALU.mult))
            if scale_shift:
                g_, b_ = scale_shift
                link(V.tensor_tensor(to, to, g_[:].unsqueeze(1).to_broadcast([P, TILES, H]), ALU.mult))
                link(V.tensor_tensor(to, to, b_[:].unsqueeze(1).to_broadcast([P, TILES, H]), ALU.add))
            else:
                link(V.tensor_scalar(to, to, 0.0, None, ALU.max))

        def dve_link(dve, ins):
            count[0] += 1
            ins.then_inc(s_dve, 1)
            dve.wait_ge(s_dve, count[0])

        def gather_ids(dve, bufs, sums_zeroed_or_added, value, col, by_dst_too, segments, ready):
            gi_s, gi_d, seg = bufs[0:3]
            V = nc.vector
            dve.wait_ge(sums_zeroed_or_added, value)
            V.tensor_copy(gi_s[:], src_f[:, bass.ds(col, 4)])
            if by_dst_too:
                V.tensor_copy(gi_d[:], dst_f[:, bass.ds(col, 4)])
            V.tensor_copy(seg[:], segments[:, bass.ds(col, 4)]).then_inc(ready, 1)

        def merge(dve, bufs, seg_across, n, chain, base, ids_ready, eq_ready):
            _, _, seg, same, before, nbef, away, sidx, ps_seg = bufs
            V = nc.vector
            dve.wait_ge(seg_across, n + 1)
            dve.wait_ge(ids_ready, n + 1)
            V.tensor_tensor(same[:], ps_seg[:], seg[:].unsqueeze(2).to_broadcast([P, 4, P]), ALU.is_equal).then_inc(chain, 1)
            V.tensor_tensor(away[:], dump[:], seg[:], ALU.subtract)
            dve.wait_ge(chain, base + 1)
            V.tensor_tensor(before[:], same[:], tri[:].unsqueeze(1).to_broadcast([P, 4, P]), ALU.mult).then_inc(chain, 1)
            dve.wait_ge(chain, base + 2)
            V.tensor_reduce(nbef[:], before[:], AX.X, ALU.add).then_inc(chain, 1)
            dve.wait_ge(chain, base + 3)
            V.scalar_tensor_tensor(away[:], nbef[:], 0.0, away[:], ALU.is_gt, ALU.mult).then_inc(chain, 1)
            dve.wait_ge(chain, base + 4)
            ins = V.tensor_tensor(sidx, away[:], seg[:], ALU.add)
            if eq_ready is not None:
                ins.then_inc(eq_ready, 1)

        def ids_across(pe, ps_seg, seg, ready, n, done):
            pe.wait_ge(ready, n)
            for c in range(4):
                last = nc.tensor.matmul(ps_seg[:, c, :], seg[:, c:c + 1].to_broadcast([P, P]), ident[:],
                                        start=True, stop=True)
            last.then_inc(done, 1)

        def zero_sums(pool, zero, signal):
            for r in range(4):
                pool.dma_start(sums[r].rearrange("(p t) c -> p (t c)", p=P), zero[:]).then_inc(signal, 16)

        windows = ctx.enter_context(ExitStack())
        stage[0] = windows
        gstart_f = sb("gstart_f", [P, GT])
        widx = sb("widx", [P, GT, WROWS], I32)
        NW = GT * WROWS * RE
        win = sb("win", [P, GT, WROWS, 2 * RE], I32)
        with ExitStack() as st:
            stage[0] = st
            first_i = sb("first_i", [P, ROWS_E], I32)
            first_f = first_i[:].bitcast(F32)
            junk = sb("junk", [P, ROWS_E], F16)
            gstart = sb("gstart", [P, GT], I32)
            grow = sb("grow", [P, GT])
            jrow = sb("jrow", [P, WROWS])
            tmp = sb("tmp", [P, TILES, H])
            rstd = sb("rstd", [P, TILES, 1])
            mult = sb("mult", [P, TILES, 1])
            zt = sb("zt", [T, NPAD], I32)
            zhot = zt[:].bitcast(F32)
            etab = sb("etab", [T, 2 * G])
            embT = sb("embT", [G, T])
            adT = sb("adT", [G, G])
            zz = sb("zz", [P, TILES, 2 * G])
            drow = sb("drow", [P, TILES, DW])
            src_i = sb("src_i", [P, CHUNKS], I32)
            dst_i = sb("dst_i", [P, CHUNKS], I32)
            dis = sb("dis", [P, CHUNKS])
            act_in = sb("act_in", [P, CHUNKS])
            zero = sb("zero", [P, (ROWS // P) * W])
            ps_z = pb("ps_z", [P, 7, 2 * G])
            ps_e = pb("ps_e", [P, 512])

            block = st.enter_context(nc.Block())

            @block.sync
            def _(sp):
                sp.dma_start(first_i[:], dst_first.partition_broadcast(P)).then_inc(c_load, 16)
                sp.dma_start(xs[:], tiles(x)).then_inc(s_load, 16)
                sp.dma_start(mult[:, :, 0], mult_n).then_inc(s_load, 16)
                sp.dma_start(gam[:], gamma.partition_broadcast(P)).then_inc(s_load, 16)
                sp.dma_start(bet[:], beta.partition_broadcast(P)).then_inc(s_load, 16)
                sp.dma_start(zt[:], types.partition_broadcast(T)).then_inc(s_load, 16)
                sp.dma_start(embT[:], emb_t).then_inc(s_load, 16)
                sp.dma_start(adT[:], adapt_t).then_inc(s_load, 16)
                sp.dma_start(etab[:, 0:G], emb).then_inc(s_load, 16)
                sp.dma_start(src_i[:], src).then_inc(s_load, 16)
                sp.dma_start(dst_i[:], dst).then_inc(s_load, 16)
                sp.dma_start(dis[:], dist).then_inc(s_load, 16)
                sp.wait_ge(s_rows, 2)
                sp.dma_start(tiles(by_dst[:, :]), drow[:]).then_inc(s_tab, 16)
                sp.dma_start(tiles(by_src[:, :]), zz[:, :, 0:G]).then_inc(s_tab, 16)
                sp.dma_start(tiles(u_tab[:, :]), tmp[:]).then_inc(s_tab, 16)
                sp.wait_ge(s_tab, 48)
            @block.gpsimd
            def _(pool):
                pool.iota(gstart[:], [[P * GD, GT]], base=0, channel_multiplier=GD).then_inc(c_io, 1)
                pool.iota(widx[:, 0, :], [[1, WROWS]], base=0, channel_multiplier=0).then_inc(c_io, 1)
                pool.iota(pidx[:], [[0, 1]], base=0, channel_multiplier=1).then_inc(s_const, 1)
                pool.memset(ident[:], 0.0).then_inc(s_const, 1)
                pool.memset(tri[:], 1.0).then_inc(s_const, 1)
                pool.wait_ge(s_const, 3)
                pool.affine_select(out=ident[:], in_=ident[:], compare_op=ALU.not_equal, fill=1.0, base=0,
                                   pattern=[[-1, P]], channel_multiplier=1).then_inc(s_const, 1)
                pool.affine_select(out=tri[:], in_=tri[:], compare_op=ALU.is_gt, fill=0.0, base=0,
                                   pattern=[[-1, P]], channel_multiplier=1).then_inc(s_const, 1)

                pool.wait_ge(s_zero, 1)
                zero_sums(pool, zero, s_add)
                pool.wait_ge(c_idx, 1)
                for t in range(GT):
                    for j in range(WROWS):
                        pool.indirect_dma_start(win[:, t, j, :], None, edge_rows,
                                                bass.IndirectOffsetOnAxis(ap=widx[:, t, j:j + 1], axis=0)).then_inc(c_win, 16)
                pool.wait_ge(s_add, 64)
            @block.scalar
            def _(act):
                act.wait_ge(s_ang, 1)
                nc.scalar.activation(act_in[:], dis[:], ACT.Sin).then_inc(s_sin, 1)
                act.wait_ge(s_var, 1)
                nc.scalar.activation(rstd[:], row2[:], ACT.Sqrt, bias=eps[:]).then_inc(s_sqrt, 1)
            @block.tensor
            def _(pe):
                pe.wait_ge(s_load, 16 * len(loads))
                pe.wait_ge(s_const, 5)
                nc.tensor.matmul(ps_e[0:T, 0:G], embT[:], adT[:], start=True, stop=True).then_inc(s_e2, 1)
                pe.wait_ge(s_e2c, 1)
                for k in range(TILES // 7):
                    if k:
                        pe.wait_ge(s_zc, k)
                    for j in range(7):
                        t = 7 * k + j
                        last = nc.tensor.matmul(ps_z[:, j, :], zhot[:, t * P:(t + 1) * P], etab[:], start=True, stop=True)
                    last.then_inc(s_z, 1)

            @block.vector
            def _(dve):
                V = nc.vector
                link = lambda ins: dve_link(dve, ins)

                V.memset(zero[:], 0.0).then_inc(s_zero, 1)
                V.memset(eps[:], EPS)
                link(V.memset(drow[:], 0.0))
                dve.wait_ge(c_io, 2)
                V.tensor_copy(jrow[:], widx[:, 0, :])
                link(V.tensor_copy(gstart_f[:], gstart[:]))
                dve.wait_ge(c_load, 16)
                link(V.tensor_copy(first_f, first_i[:]))
                for t in range(GT):
                    link(V.tensor_scalar(junk[:], first_f, gstart_f[:, t:t + 1], None, ALU.is_lt, ALU.add,
                                         accum_out=grow[:, t:t + 1]))
                link(V.tensor_scalar(grow[:], grow[:], -1.0, 0.0, ALU.add, ALU.max))
                V.tensor_tensor(widx[:], jrow[:].unsqueeze(1).to_broadcast([P, GT, WROWS]),
                                grow[:].unsqueeze(2).to_broadcast([P, GT, WROWS]), ALU.add).then_inc(c_idx, 1)
                dve.wait_ge(s_load, 16 * len(loads))
                dve.wait_ge(s_const, 5)
                V.tensor_scalar(cut[:], dis[:], CUTOFF, 0.5, ALU.is_lt, ALU.mult)
                link(V.tensor_scalar(act_in[:], dis[:], CUTOFF, None, ALU.min))
                V.tensor_scalar(dis[:], act_in[:], -PI / CUTOFF, PI / 2, ALU.mult, ALU.add).then_inc(s_ang, 1)
                V.tensor_copy(src_f[:], src_i[:])
                V.tensor_copy(dst_f[:], dst_i[:])
                link(V.tensor_copy(pidx_f[:], pidx[:]))
                dve.wait_ge(s_sin, 1)
                link(V.tensor_scalar(act_in[:], act_in[:], 1.0, None, ALU.add))
                link(V.tensor_tensor(cut[:], cut[:], act_in[:], ALU.mult))
                for c in range(4):
                    link(V.tensor_scalar(dump[:, c:c + 1], pidx_f[:], float(DUMP), None, ALU.add))
                link(V.tensor_scalar(zhot, zt[:], float(T - 1), None, ALU.min))
                link(V.tensor_scalar(zhot, zhot, pidx_f[0:T, :], None, ALU.is_equal))
                dve.wait_ge(s_e2, 1)
                V.tensor_copy(etab[:, G:2 * G], ps_e[0:T, 0:G]).then_inc(s_e2c, 1)
                link(V.tensor_copy(tmp[:], xs[:]))
                layernorm(dve, hs_n[:], tmp, rstd)
                V.tensor_tensor(drow[:, :, 0:H], hs_n[:], mult[:].to_broadcast([P, TILES, H]), ALU.mult)
                V.tensor_copy(drow[:, :, H + G:H + G + 1], mult[:])
                for k in range(TILES // 7):
                    dve.wait_ge(s_z, k + 1)
                    V.tensor_copy(zz[:, 7 * k:7 * k + 7, :], ps_z[:]).then_inc(s_zc, 1)
                dve.wait_ge(s_zc, TILES // 7)
                V.tensor_copy(drow[:, :, H:H + G], zz[:, :, G:2 * G]).then_inc(s_rows, 1)
                V.memset(tmp[:], 1.0).then_inc(s_rows, 1)


        with ExitStack() as both:
            stage[0] = both
            e_low = sb("e_low", [P, WCH, GT * P])
            e_key = sb("e_key", [P, WCH, GT * P])
            cols = sb("cols", [P, GCOLS], F16)
            place = sb("place", [P, BATCHES, BATCH])
            facts = sb("facts", [P, CHUNKS, 8], F16)
            in_range = sb("in_range", [P, 1])
            most = sb("most", [P, 1])
            over = sb("over", [P, TILES, XP])
            over2 = sb("over2", [P, XP])
            minus = sb("minus", [P, 1])
            onesf = sb("onesf", [P, P])
            zero16 = sb("zero16", [P, P], F16)
            ident16 = sb("ident16", [P, P], F16)
            mult_hl = sb("mult_hl", [P, TILES, 2], F16)

            with ExitStack() as st:
                stage[0] = st
                parts = sb("parts", [P, 2 * NW], I32)
                low_i, tile_i = (parts[:, h * NW:(h + 1) * NW].rearrange("p (t j e) -> p t j e", t=GT, j=WROWS) for h in range(2))
                low_f, tile_f = (parts[:, h * NW:(h + 1) * NW].bitcast(F32).rearrange("p (t e) -> p t e", t=GT) for h in range(2))
                key = sb("key", [P, GT, WROWS * RE])
                mult1 = sb("mult1", [P, TILES])
                square = sb("square", [P, TILES])
                rel = e_low[:].rearrange("p c g -> p (c g)").rearrange("p (t e) -> p t e", t=GT)
                cols_i = sb("cols_i", [P, GCOLS], I32)
                keep = sb("keep", [P, CHUNKS], F16)
                keep_b = keep[:].rearrange("p (b i) -> p b i", i=BATCH)
                ids_i = sb("ids_i", [P, CHUNKS], I32)
                bits = sb("bits", [P, CHUNKS], I32)
                below = sb("below", [P, P], F16)
                ones16 = sb("ones16", [P, P], F16)
                banks = [pb(f"rank{k}", [P, 512]) for k in range(5)]
                ps_tr = [pb(f"ps_tr{k}", [P, 4, P]) for k in range(2)]
                NTR = GT * WCH * 2
                block = st.enter_context(nc.Block())

                @block.sync
                def _(sp):
                    sp.dma_start(mult1[:], mult_n).then_inc(c_load, 16)

                @block.gpsimd
                def _(pool):
                    pool.iota(cols_i[:], [[1, GCOLS]], base=0, channel_multiplier=0).then_inc(c_io, 1)
                    pool.iota(ids_i[:], [[1, CHUNKS]], base=0, channel_multiplier=0).then_inc(r_io, 1)
                    pool.memset(below[:], 1.0).then_inc(r_io, 1)
                    pool.wait_ge(r_io, 2)
                    pool.affine_select(out=below[:], in_=below[:], compare_op=ALU.is_gt, fill=0.0, base=0,
                                       pattern=[[1, P]], channel_multiplier=-1).then_inc(r_io, 1)

                @block.tensor
                def _(pe):
                    pe.wait_ge(r_io, 3)
                    pe.wait_ge(r_keep, 1)
                    for i in range(BATCH):
                        to = banks[i // 2][:, (i % 2) * BATCHES:(i % 2 + 1) * BATCHES]
                        for j in range(i):
                            nc.tensor.matmul(to, ones16[:], keep_b[:, :, j], start=(j == 0), stop=False)
                        nc.tensor.matmul(to, below[:], keep_b[:, :, i], start=(i == 0), stop=True)
                    for j in range(BATCH):
                        last = nc.tensor.matmul(banks[4][:, 0:BATCHES], ones16[:], keep_b[:, :, j], start=(j == 0),
                                                stop=(j == BATCH - 1))
                    last.then_inc(r_rank, 1)
                    pe.wait_ge(c_key, 1)
                    n = 0
                    for k in range(NTR // 3):
                        if k >= 2:
                            pe.wait_ge(c_trc, k - 1)
                        for j in range(3):
                            arr, t = divmod(n // WCH, GT)
                            c = n % WCH
                            last = nc.tensor.transpose(ps_tr[k % 2][:, j, :], (low_f, key)[arr][:, t, c * P:(c + 1) * P], ident[:])
                            n += 1
                        last.then_inc(c_tr, 1)

                @block.vector
                def _(dve):
                    V = nc.vector
                    link = lambda ins: dve_link(dve, ins)
                    V.memset(ones16[:], 1.0)
                    V.memset(minus[:], -float(EXACT))
                    V.memset(onesf[:], 1.0)
                    V.memset(zero16[:], 0.0)
                    V.memset(over[:], 0.0)
                    dve.wait_ge(c_io, 3)
                    V.tensor_copy(cols[:], cols_i[:])
                    V.tensor_copy(ident16[:], ident[:])
                    dve.wait_ge(c_load, 32)
                    link(V.tensor_tensor(square[:], mult1[:], mult1[:], ALU.mult))
                    link(V.tensor_scalar(square[:], square[:], MULT_MAX ** 2, None, ALU.is_le))
                    link(V.tensor_reduce(in_range[:], square[:], AX.X, ALU.add))
                    link(V.tensor_scalar(mult1[:], mult1[:], MULT_SCALE, None, ALU.mult))
                    link(V.tensor_copy(mult_hl[:, :, 0], mult1[:]))
                    V.tensor_tensor(mult_hl[:, :, 1], mult1[:], mult_hl[:, :, 0], ALU.subtract)
                    V.tensor_scalar(keep[:], cut[:], 0.0, None, ALU.not_equal).then_inc(r_keep, 1)
                    dve.wait_ge(r_io, 3)
                    V.tensor_copy(facts[:, :, 0], ids_i[:])
                    link(V.tensor_copy(facts[:, :, 3], pidx_f[:].to_broadcast([P, CHUNKS])))
                    for k, ids in enumerate((src_f, dst_f)):
                        link(V.tensor_copy(ids_i[:], ids[:]))
                        link(V.tensor_scalar(bits[:], ids_i[:], 7, None, ALU.logical_shift_right))
                        link(V.tensor_copy(facts[:, :, 1 + k], bits[:]))
                        link(V.tensor_scalar(bits[:], ids_i[:], P - 1, None, ALU.bitwise_and))
                        link(V.tensor_copy(facts[:, :, 4 + k], bits[:]))
                    link(V.tensor_copy(facts[:, :, 6], cut[:]))
                    link(V.tensor_tensor(facts[:, :, 7], cut[:], facts[:, :, 6], ALU.subtract))
                    dve.wait_ge(r_rank, 1)
                    for k in range(BATCH // 2):
                        V.scalar_tensor_tensor(place[:, :, 2 * k:2 * k + 2].rearrange("p b i -> p i b"),
                                               banks[k][:, 0:2 * BATCHES].rearrange("p (i b) -> p i b", i=2), 1.0,
                                               keep_b[:, :, 2 * k:2 * k + 2].rearrange("p b i -> p i b"), ALU.add, ALU.mult)
                    link(V.tensor_reduce(most[:], banks[4][:, 0:BATCHES], AX.X, ALU.max))
                    link(V.tensor_scalar(place[:], place[:], -1.0, None, ALU.add))
                    link(V.tensor_scalar(most[:], most[:], float(ROOM), None, ALU.is_le))
                    dve.wait_ge(c_win, 16 * GT * WROWS)
                    w = win[:].rearrange("p t j e -> p (t j) e")
                    in_rows = lambda ap: ap.rearrange("p t (j e) -> p (t j) e", e=RE)
                    V.tensor_scalar(low_i.rearrange("p t j e -> p (t j) e"), w[:, :, 0:RE], P - 1, None, ALU.bitwise_and)
                    V.tensor_scalar(tile_i.rearrange("p t j e -> p (t j) e"), w[:, :, 0:RE], 7, None, ALU.logical_shift_right)
                    link(V.tensor_copy(in_rows(rel), w[:, :, RE:2 * RE]))
                    V.tensor_copy(low_f, low_i.rearrange("p t j e -> p t (j e)"))
                    V.tensor_copy(tile_f, tile_i.rearrange("p t j e -> p t (j e)"))
                    link(V.tensor_tensor(rel, rel, gstart_f[:].unsqueeze(2).to_broadcast([P, GT, WROWS * RE]), ALU.subtract))
                    V.scalar_tensor_tensor(key[:], rel, float(TILES), tile_f, ALU.mult, ALU.add).then_inc(c_key, 1)
                    n = 0
                    for k in range(NTR // 3):
                        dve.wait_ge(c_tr, k + 1)
                        arr, t = divmod(n // WCH, GT)
                        here = ps_tr[k % 2][:, 0:WCH, :]
                        V.tensor_copy((e_low, e_key)[arr][:, :, t * P:(t + 1) * P], here).then_inc(c_trc, 1)
                        n += WCH
                    dve.wait_ge(c_trc, NTR // 3)

            stage[0] = both
            hot_low = sb("hot_low", [P, DEPTH, TURN * WCH, P], F16)
            hot_key = sb("hot_key", [P, DEPTH, TURN * WCH, GCOLS], F16)
            full = sb("full", [P, 2, TILES, P], F8)
            flip = sb("flip", [P, 2, 4 * P], F16)
            deg1 = sb("deg1", [P, FLIPS])
            deg_parts = sb("deg_parts", [P, TILES, FLIPS])
            spare = sb("spare", [P, NPAD], F16)[:]
            check2 = sb("check2", [P, 3])
            ok2 = sb("ok2", [P, 3])
            w1s = sb("w1s", [R, H])
            b1s = sb("b1s", [H, 1])
            w2s = sb("w2s", [H + 1, H])
            attr_sb = sb("attr_sb", [R, 4 * P])
            hid = sb("hid", [H + 1, 4 * P])
            hot = sb("hot", [P, 2 * BATCH, ROOM], F16)
            moved = sb("moved", [P, 4, 8])
            kept_f = sb("kept_f", [P, 4, IDS])
            kept = sb("kept", [P, 2, 4, IDS], I32)
            cut_k = sb("cut_k", [P, 2, 4, 1])
            seg_k = sb("seg_k", [P, 2, 4])
            ag = sb("ag", [P, 2, 4, R])
            dg = sb("dg", [P, 2, 4, DW])
            sg = sb("sg", [P, 2, 4, G])
            same = sb("same", [P, 4, P])
            before = sb("before", [P, 4, P])
            nbef = sb("nbef", [P, 4])
            away = sb("away", [P, 4])
            sidx = sb("sidx", [P, 2, 4], I32)
            hmc = sb("hmc", [P, 4, H])
            ad = sb("ad", [P, 4, G])
            ads = sb("ads", [P, 4, 1])
            gate_a = sb("gate_a", [P, 4, H])
            msg = sb("msg", [P, 4, H])
            outrow = sb("outrow", [P, 2, 4, W])
            counts = [pb(f"counts{k}", [P, 512]) for k in range(2 * TURN)]
            ps_tot = pb("ps_tot", [P, 512])[:, 0:2 * TILES]
            ps_flip = pb("ps_flip", [P, 512])
            ps_ok = ps_flip[:, 0:3]
            bank_x, bank_y = pb("bank_x", [P, 512]), pb("bank_y", [P, 512])
            ps_seg = bank_x[:].rearrange("p (c e) -> p c e", c=4)
            ps_gate = bank_x[:, 0:4 * H].rearrange("p (c h) -> p c h", c=4)
            ps_moved = bank_y[:, 0:32].rearrange("p (c k) -> p c k", c=4)
            ps_at = bank_y[:].rearrange("p (c e) -> p c e", c=4)
            ps_h = bank_y
            ps_sum = bank_y[:, 0:4 * H].rearrange("p (c h) -> p c h", c=4)

            def gathered(q, b):
                return q * 96 + (96 if b else 192)

            def over_all(engine, turn, point):
                def block_(b, slot, first):
                    for t in range(TURNS):
                        turn(b, slot, first, t)
                        point(b * 2 + t // TPP, t // TPP, t % TPP, True)
                block_(0, 0, True)
                with engine.Fori(0, (TILES - 1) // 2) as k:
                    b = engine.snap(k * 2 + 1)
                    block_(b, 1, False)
                    block_(b + 1, 0, False)
                for q in range(2 * TILES, PAIRS):
                    for k in range(TPP):
                        point(q, q % 2, k, q + 1 < PAIRS)

            block = both.enter_context(nc.Block())

            @block.sync
            def _(sp):
                sp.dma_start(w1s[:], w1t).then_inc(s_load, 16)
                sp.dma_start(b1s[:], b1).then_inc(s_load, 16)
                sp.dma_start(w2s[:], w2e).then_inc(s_load, 16)
                sp.sem_inc(c_free, 1)

                def turn(b, slot, first, t):
                    if t == TURNS - 1:
                        sp.wait_ge(c_took, b * TURNS + TURNS)
                        sp.sem_inc(s_go, 1)
                        sp.dma_start(counts_d[at(b)].rearrange("b p c -> p (b c)"),
                                     full[:, slot].rearrange("p t c -> p (t c)").bitcast(U8)).then_inc(c_stored[slot], 16)
                        sp.wait_ge(c_stored[slot], b * 8 + (8 if slot else 16))
                        sp.sem_inc(c_free, 1)
                over_all(sp, turn, lambda q, b, k, more: None)
                sp.wait_ge(c_stored[0], 16 * (TILES // 2 + 1))
                sp.wait_ge(c_stored[1], 16 * (TILES // 2))

            @block.gpsimd
            def _(pool):
                def gathers(q, b):
                    pool.wait_ge(a_idx, q + 1)
                    pool.sem_inc(s_mark, 1)
                    for c in range(4):
                        for k, (to, table) in enumerate(((ag, attr), (sg, by_src[:, :]), (dg, by_dst[:, :]))):
                            pool.indirect_dma_start(to[:, b, c, :], None, table,
                                                    bass.IndirectOffsetOnAxis(ap=kept[:, b, c, k:k + 1], axis=0)).then_inc(p_gath[b], 16)

                def point(q, b, k, more):
                    if k < TPP - 1:
                        return
                    if more:
                        gathers(q + 1, 1 - b)
                    pool.wait_ge(a_out, q + 1)
                    pool.wait_ge(s_add, q * 64 + 64)
                    pool.sem_inc(s_mark, 1)
                    for c in range(4):
                        pool.indirect_dma_start(sums[c][:, :], bass.IndirectOffsetOnAxis(ap=sidx[:, b, c:c + 1], axis=0),
                                                outrow[:, b, c, :], None, compute_op=ALU.add).then_inc(s_add, 16)
                gathers(0, 0)
                over_all(pool, lambda *_: None, point)
                pool.wait_ge(s_add, 64 * (PAIRS + 1))

            @block.scalar
            def _(act):
                def turn(b, slot, first, t):
                    n = b * TURNS + t
                    if not first and 0 < 2 * t - 1 < FLIPS:
                        take_flip(b - 1, 2 * t - 1)
                    act.wait_ge(c_cnt, n + 1)
                    if t == 0 and not first:
                        act.wait_ge(c_free, b)
                    act.sem_inc(c_mark, 1)
                    for g in range(TURN):
                        j = t * TURN + g
                        bank = counts[(t % 2) * TURN + g][:, 0:GCOLS]
                        last = nc.scalar.activation(full[:, slot, :, GD * j:GD * j + GD], bank.rearrange("p (d s) -> p s d", d=GD),
                                                    ACT.Copy, saturate=False)
                    last.then_inc(c_took, 1)
                    if not first and 2 * t < FLIPS:
                        take_flip(b - 1, 2 * t)
                    if not first and t % 2 == 0:
                        excess(b - 1, 1 - slot, t // 2)

                def take_flip(b, j):
                    n = min(4, TILES - 4 * j) * P
                    act.wait_ge(c_flip, b * FLIPS + (j + 1))
                    nc.scalar.activation(flip[:, j % 2, 0:n], ps_flip[:, 0:n], ACT.Copy, accum_out=deg1[:, j:j + 1]).then_inc(c_flipc, 1)
                    if j == FLIPS - 1:
                        act.wait_ge(c_flipc, b * FLIPS + FLIPS)
                        nc.scalar.activation(deg_parts[:, at(b), :].rearrange("p a b -> p (a b)"), deg1[:], ACT.Copy).then_inc(c_degc, 1)

                def excess(b, slot, piece):
                    act.wait_ge(c_took, b * TURNS + TURNS)
                    act.sem_inc(c_mark, 1)
                    part_of = full[:, slot].rearrange("p t c -> p (t c)")[:, piece * XC:(piece + 1) * XC]
                    nc.scalar.activation(spare[:, piece * XC:(piece + 1) * XC], part_of, ACT.Relu, bias=minus[:],
                                         accum_out=over2[:, piece:piece + 1]).then_inc(c_over, 1)
                    if piece == XP - 1:
                        act.wait_ge(c_over, b * XP + XP)
                        nc.scalar.activation(over[:, at(b), :].rearrange("p a b -> p (a b)"), over2[:], ACT.Copy).then_inc(c_over2, 1)

                def point(q, b, k, more):
                    if k == 1:
                        act.wait_ge(p_tr, q + 1)
                        nc.scalar.activation(attr_sb[:].rearrange("r (c e) -> r c e", c=4), ps_at[0:R], ACT.Copy).then_inc(p_atc, 1)
                        act.wait_ge(a_h, q + 1)
                        nc.scalar.activation(hid[0:H, :], ps_h[0:H, :], ACT.Silu, bias=b1s[:]).then_inc(a_hid, 1)
                    if k == 3:
                        act.wait_ge(a_sum, q + 1)
                        nc.scalar.activation(outrow[:, b, :, 0:H], ps_sum, ACT.Copy).then_inc(a_out, 1)

                act.wait_ge(s_load, 16 * (len(loads) + 3))
                over_all(act, turn, point)
                for piece in range(XP):
                    excess(TILES - 1, 0, piece)
                for j in range(FLIPS):
                    take_flip(TILES - 1, j)

            @block.tensor
            def _(pe):
                def weigh(b, j):
                    for i in range(min(4, TILES - 4 * j)):
                        k = 4 * j + i
                        nc.tensor.matmul(ps_tot[:, 2 * k:2 * k + 2], flip[:, j % 2, i * P:(i + 1) * P],
                                         mult_hl[:, at(b), :].rearrange("p a h -> p (a h)"), start=False, stop=False)

                def flips(b, slot, j):
                    if j == 0:
                        pe.wait_ge(c_took, b * TURNS + TURNS)
                    else:
                        pe.wait_ge(c_flipc, b * FLIPS + j)
                    pe.sem_inc(c_turn, 1)
                    if j < FLIPS:
                        for i in range(min(4, TILES - 4 * j)):
                            last = nc.tensor.matmul(ps_flip[:, i * P:(i + 1) * P], full[:, slot, 4 * j + i, :], ident16[:],
                                                    start=True, stop=True)
                        last.then_inc(c_flip, 1)
                    if j > 0:
                        weigh(b, j - 1)

                def turn(b, slot, first, t):
                    n = b * TURNS + t
                    if not first and 0 < 2 * t - 1 <= FLIPS:
                        flips(b - 1, 1 - slot, 2 * t - 1)
                    pe.wait_ge(c_one, n + 1)
                    if not (first and t < 2):
                        pe.wait_ge(c_took, n - 1)
                    for g in range(TURN):
                        for c in range(WCH):
                            last = nc.tensor.matmul(counts[(t % 2) * TURN + g][:, 0:GCOLS], hot_low[:, t % DEPTH, g * WCH + c, :],
                                                    hot_key[:, t % DEPTH, g * WCH + c, :], start=(c == 0), stop=(c == WCH - 1))
                    last.then_inc(c_cnt, 1)
                    if not first and 2 * t <= FLIPS:
                        flips(b - 1, 1 - slot, 2 * t)

                def move(q):
                    pe.wait_ge(p_hot, q + 1)
                    for c in range(4):
                        for i in range(BATCH):
                            k = (c // 2) * BATCH + i
                            last = nc.tensor.matmul(ps_moved[:, c, :], hot[:, k, (c % 2) * P:(c % 2 + 1) * P],
                                                    facts[:, at(q * (2 * BATCH) + k), :].rearrange("p a k -> p (a k)"),
                                                    start=(i == 0), stop=(i == BATCH - 1))
                    last.then_inc(p_pay, 1)

                def point(q, b, k, more):
                    if k == 0:
                        if not (isinstance(q, int) and q == 0):
                            pe.wait_ge(a_out, q)
                        ids_across(pe, ps_seg, seg_k[:, b], a_idx, q + 1, a_seg)
                        if more:
                            move(q + 1)
                    if k == 1:
                        if more:
                            pe.wait_ge(p_pc, q * 2 + 3)
                        pe.wait_ge(p_gath[b], gathered(q, b))
                        pe.sem_inc(s_turn, 1)
                        for c in range(4):
                            last = nc.tensor.transpose(ps_at[0:R, c, :], ag[:, b, c, :], ident[:])
                        last.then_inc(p_tr, 1)
                        pe.wait_ge(p_atc, q + 1)
                        pe.sem_inc(s_turn, 1)
                        nc.tensor.matmul(ps_h[0:H, :], w1s[:], attr_sb[:], start=True, stop=True).then_inc(a_h, 1)
                        pe.wait_ge(a_hid, q + 1)
                        pe.wait_ge(a_dve, q * 6 + 1)
                        for c in range(4):
                            last = nc.tensor.matmul(ps_gate[:, c, :], hid[:, c * P:(c + 1) * P], w2s[:], start=True, stop=True)
                        last.then_inc(a_gate, 1)
                    if k == 3:
                        pe.wait_ge(a_msg, q + 1)
                        for c in range(4):
                            last = nc.tensor.matmul(ps_sum[:, c, :], same[:, c, :], msg[:, c, :], start=True, stop=True)
                        last.then_inc(a_sum, 1)

                pe.wait_ge(s_load, 16 * (len(loads) + 3))
                pe.wait_ge(s_ones, 2)
                nc.tensor.matmul(ps_tot, zero16[:], zero16[:, 0:2 * TILES], start=True, stop=False)
                move(0)
                over_all(pe, turn, point)
                for j in range(FLIPS + 1):
                    flips(TILES - 1, 0, j)
                nc.tensor.matmul(ps_tot, zero16[:], zero16[:, 0:2 * TILES], start=False, stop=True).then_inc(c_tot, 1)
                pe.wait_ge(c_dve, 1)
                nc.tensor.matmul(ps_ok, onesf[:], check2[:], start=True, stop=True).then_inc(c_sum, 1)

            @block.vector
            def _(dve):
                V = nc.vector
                link = lambda ins: dve_link(dve, ins)
                flat = place[:].rearrange("p b i -> p (b i)")
                V.memset(outrow[:], 0.0).then_inc(s_ones, 1)
                V.memset(hid[:], 1.0).then_inc(s_ones, 1)

                def turn(b, slot, first, t):
                    n = b * TURNS + t
                    if not (first and t < DEPTH):
                        dve.wait_ge(c_cnt, n - DEPTH + 1)
                    for g in range(TURN):
                        col = b * GPB + (t * TURN + g)
                        if not first:
                            col = dve.snap(col)
                        for c in range(WCH):
                            V.tensor_scalar(hot_key[:, t % DEPTH, g * WCH + c, :], cols[:], e_key[:, c, at(col)], None, ALU.is_equal)
                            last = V.tensor_scalar(hot_low[:, t % DEPTH, g * WCH + c, :], cols[:, 0:P], e_low[:, c, at(col)], None, ALU.is_equal)
                    last.then_inc(c_one, 1)

                def places(q):
                    for k in range(2 * BATCH):
                        last = V.tensor_scalar(hot[:, k, :], cols[:, 0:ROOM], flat[:, at(q * (2 * BATCH) + k)], None, ALU.is_equal)
                    last.then_inc(p_hot, 1)

                def ids(q, b):
                    dve.wait_ge(p_pay, q + 1)
                    V.tensor_copy(moved[:], ps_moved).then_inc(p_pc, 1)
                    dve.wait_ge(p_pc, q * 2 + 1)
                    V.scalar_tensor_tensor(kept_f[:], moved[:, :, 0:IDS], float(P), moved[:, :, IDS:2 * IDS], ALU.mult, ALU.add).then_inc(p_pc, 1)
                    V.tensor_tensor(cut_k[:, b, :, 0], moved[:, :, 6], moved[:, :, 7], ALU.add)
                    dve.wait_ge(p_pc, q * 2 + 2)
                    V.tensor_copy(seg_k[:, b], kept_f[:, :, 1])
                    V.tensor_copy(kept[:, b], kept_f[:]).then_inc(a_idx, 1)

                def point(q, b, k, more):
                    if k == 0 and more:
                        places(q + 1)
                    if k == 1:
                        if more:
                            ids(q + 1, 1 - b)
                        if not (isinstance(q, int) and q == 0):
                            dve.wait_ge(s_add, q * 64)
                        merge(dve, (None, None, seg_k[:, b], same, before, nbef, away, sidx[:, b], ps_seg), a_seg, q, a_dve, q * 6,
                              a_idx, None)
                    if k == 2:
                        dve.wait_ge(p_gath[b], gathered(q, b))
                        V.tensor_tensor(hmc[:], dg[:, b, :, 0:H], cut_k[:, b].to_broadcast([P, 4, H]), ALU.mult)
                        V.tensor_tensor(ad[:], sg[:, b], dg[:, b, :, H:H + G], ALU.mult).then_inc(a_dve, 1)
                        dve.wait_ge(a_dve, q * 6 + 5)
                        V.tensor_reduce(ads[:, :, 0], ad[:], AX.X, ALU.add).then_inc(a_dve, 1)
                    if k == 3:
                        dve.wait_ge(a_dve, q * 6 + 6)
                        dve.wait_ge(a_gate, q + 1)
                        V.tensor_tensor(gate_a[:], ps_gate, ads[:].to_broadcast([P, 4, H]), ALU.add).then_inc(a_mg, 1)
                        dve.wait_ge(a_mg, q + 1)
                        V.tensor_tensor(msg[:], gate_a[:], hmc[:], ALU.mult).then_inc(a_msg, 1)

                places(0)
                ids(0, 0)
                over_all(dve, turn, point)
                dve.wait_ge(c_degc, TILES)
                dve.wait_ge(c_over2, TILES)
                link(V.tensor_reduce(deg[:, :, 0], deg_parts[:], AX.X, ALU.add))
                V.tensor_copy(check2[:, 2:3], in_range[:])
                V.tensor_reduce(check2[:, 0:1], deg[:, :, 0], AX.X, ALU.add)
                V.tensor_reduce(check2[:, 1:2], over[:].rearrange("p b k -> p (b k)"), AX.X, ALU.add).then_inc(c_dve, 1)
                dve.wait_ge(c_sum, 1)
                V.tensor_scalar(ok2[:, 0:1], ps_ok[:, 0:1], float(EPAD), None, ALU.is_equal)
                link(V.tensor_scalar(ok2[:, 1:2], ps_ok[:, 1:2], 0.0, None, ALU.is_equal))
                link(V.tensor_scalar(ok2[:, 2:3], ps_ok[:, 2:3], float(NPAD), None, ALU.is_equal))
                link(V.tensor_tensor(dense_all[:], ok2[:, 0:1], ok2[:, 1:2], ALU.mult))
                link(V.tensor_copy(dense[:], dense_all[0:1, :]))
                dve.wait_ge(c_tot, 1)
                link(V.tensor_reduce(tot[:, :, 0], ps_tot.rearrange("p (t h) -> p t h", h=2), AX.X, ALU.add))
                link(V.tensor_scalar(tot[:], tot[:], 1.0 / MULT_SCALE, None, ALU.mult))
                link(V.tensor_tensor(few_all[:], most[:], dense_all[:], ALU.mult))
                link(V.tensor_tensor(few_all[:], few_all[:], ok2[:, 2:3], ALU.mult))
                link(V.tensor_copy(few[:], few_all[0:1, :]))

        windows.close()

        with ExitStack() as st:
            stage[0] = st
            tmp = sb("tmp0", [P, TILES, H])
            acc = sb("acc", [P, TILES, H])
            part = sb("part", [P, 4, TILES, H + 1])
            rstd = sb("rstd0", [P, TILES, 1])
            zero = sb("zero0", [P, (ROWS // P) * W])
            w1s = sb("w1a", [R, H])
            b1s = sb("b1a", [H, 1])
            w2s = sb("w2a", [H + 1, H])
            attr_sb = sb("attr_a", [R, 4 * P])
            hid = sb("hid_a", [H + 1, 4 * P])
            gi_d = sb("gi_d", [P, 4], I32)
            gi_s = sb("gi_s", [P, 4], I32)
            seg = sb("seg", [P, 4])
            dg = sb("dg_a", [P, 4, DW])
            sg = sb("sg_a", [P, 4, G])
            same = sb("same_a", [P, 4, P])
            before = sb("before_a", [P, 4, P])
            nbef = sb("nbef_a", [P, 4])
            away = sb("away_a", [P, 4])
            sidx = sb("sidx_a", [P, 4], I32)
            hmc = sb("hmc_a", [P, 4, H])
            ad = sb("ad_a", [P, 4, G])
            ads = sb("ads_a", [P, 4, 1])
            gate_a = sb("gate_all", [P, 4, H])
            msg = sb("msg_a", [P, 4, H + 1])
            outrow = sb("outrow_a", [P, 4, W])
            banks = [pb(f"bank{k}", [P, 512]) for k in range(4)]
            ps_seg = banks[0][:].rearrange("p (c e) -> p c e", c=4)
            ps_h = banks[1]
            ps_gate = banks[2][:, 0:4 * H].rearrange("p (c h) -> p c h", c=4)
            ps_sum = banks[3][:, 0:4 * (H + 1)].rearrange("p (c h) -> p c h", c=4)
            block = st.enter_context(nc.Block())

            @block.sync
            def _(sp):
                sp.dma_start(w1s[:], w1t).then_inc(s_load, 16)
                sp.dma_start(b1s[:], b1).then_inc(s_load, 16)
                sp.dma_start(w2s[:], w2e).then_inc(s_load, 16)

                def all_edges():
                    with sp.Fori(0, QUADS) as q:
                        sp.wait_ge(a_idx, q + (PAIRS + 1))
                        sp.dma_start(attr_sb[:], attr_t[:, bass.ds(q * (4 * P), 4 * P)]).then_inc(a_at, 16)
                    sp.wait_ge(s_add, 64 * (QUADS + PAIRS + 2))

                either(sp, few, lambda: sp.wait_ge(s_add, 64 * (PAIRS + 1)), all_edges)
                for r in range(4):
                    sp.dma_start(part[:, r], tiles(sums[r][0:NPAD, 0:H + 1])).then_inc(s_back, 16)

            @block.gpsimd
            def _(pool):
                def all_edges():
                    pool.wait_ge(s_zero, 2)
                    zero_sums(pool, zero, s_add)
                    with pool.Fori(0, QUADS) as q:
                        pool.wait_ge(a_idx, q + (PAIRS + 1))
                        pool.sem_inc(s_mark, 1)
                        for c in range(4):
                            pool.indirect_dma_start(dg[:, c, :], None, by_dst[:, :],
                                                    bass.IndirectOffsetOnAxis(ap=gi_d[:, c:c + 1], axis=0)).then_inc(a_gath, 16)
                            pool.indirect_dma_start(sg[:, c, :], None, by_src[:, :],
                                                    bass.IndirectOffsetOnAxis(ap=gi_s[:, c:c + 1], axis=0)).then_inc(a_gath, 16)
                        pool.wait_ge(a_out, q + (PAIRS + 1))
                        pool.sem_inc(s_mark, 1)
                        for c in range(4):
                            pool.indirect_dma_start(sums[c][:, :], bass.IndirectOffsetOnAxis(ap=sidx[:, c:c + 1], axis=0),
                                                    outrow[:, c, :], None, compute_op=ALU.add).then_inc(s_add, 16)

                either(pool, few, lambda: pool.sem_inc(s_mark, 1), all_edges)

            @block.scalar
            def _(act):
                def all_edges():
                    with act.Fori(0, QUADS) as q:
                        act.wait_ge(a_h, q + (PAIRS + 1))
                        nc.scalar.activation(hid[0:H, :], ps_h[0:H, :], ACT.Silu, bias=b1s[:]).then_inc(a_hid, 1)
                        act.wait_ge(a_sum, q + (PAIRS + 1))
                        nc.scalar.activation(outrow[:, :, 0:H + 1], ps_sum[:], ACT.Copy).then_inc(a_out, 1)

                act.wait_ge(s_load, 16 * (len(loads) + 6))
                either(act, few, lambda: act.sem_inc(c_mark, 1), all_edges)
                for k in range(2):
                    act.wait_ge(s_var, 2 + k)
                    nc.scalar.activation(rstd[:], row2[:], ACT.Sqrt, bias=eps[:]).then_inc(s_sqrt, 1)

            @block.tensor
            def _(pe):
                def all_edges():
                    with pe.Fori(0, QUADS) as q:
                        ids_across(pe, ps_seg, seg, a_idx, q + (PAIRS + 1), a_seg)
                        pe.wait_ge(a_at, 16 * q + 16)
                        pe.sem_inc(s_turn, 1)
                        nc.tensor.matmul(ps_h[0:H, :], w1s[:], attr_sb[:], start=True, stop=True).then_inc(a_h, 1)
                        pe.wait_ge(a_hid, q + (PAIRS + 1))
                        for c in range(4):
                            last = nc.tensor.matmul(ps_gate[:, c, :], hid[:, c * P:(c + 1) * P], w2s[:], start=True, stop=True)
                        last.then_inc(a_gate, 1)
                        pe.wait_ge(a_msg, q + (PAIRS + 1))
                        for c in range(4):
                            last = nc.tensor.matmul(ps_sum[:, c, :], same[:, c, :], msg[:, c, :], start=True, stop=True)
                        last.then_inc(a_sum, 1)

                pe.wait_ge(s_load, 16 * (len(loads) + 6))
                pe.wait_ge(s_ones, 4)
                either(pe, few, lambda: pe.sem_inc(c_turn, 1), all_edges)

            @block.vector
            def _(dve):
                V = nc.vector
                link = lambda ins: dve_link(dve, ins)
                V.memset(zero[:], 0.0).then_inc(s_zero, 1)
                V.memset(outrow[:], 0.0).then_inc(s_ones, 1)
                V.memset(hid[:], 1.0).then_inc(s_ones, 1)

                def all_edges():
                    V.memset(tot[:], 0.0).then_inc(s_tot, 1)
                    bufs = (gi_s, gi_d, seg, same, before, nbef, away, sidx[:], ps_seg)
                    with dve.Fori(0, QUADS) as q:
                        col = dve.snap(q * 4)
                        gather_ids(dve, bufs, s_add, q * 64 + 64 * (PAIRS + 2), col, True, src_f, a_idx)
                        merge(dve, bufs, a_seg, q + PAIRS, a_dve, q * 6 + 6 * PAIRS, a_idx, None)
                        dve.wait_ge(a_gath, q * 128 + 128)
                        V.tensor_tensor(hmc[:], dg[:, :, 0:H], cut[:, bass.ds(col, 4)].unsqueeze(2).to_broadcast([P, 4, H]), ALU.mult)
                        V.tensor_copy(msg[:, :, H:H + 1], dg[:, :, H + G:H + G + 1])
                        V.tensor_tensor(ad[:], sg[:], dg[:, :, H:H + G], ALU.mult).then_inc(a_dve, 1)
                        dve.wait_ge(a_dve, q * 6 + (6 * PAIRS + 5))
                        V.tensor_reduce(ads[:, :, 0], ad[:], AX.X, ALU.add).then_inc(a_dve, 1)
                        dve.wait_ge(a_dve, q * 6 + (6 * PAIRS + 6))
                        dve.wait_ge(a_gate, q + (PAIRS + 1))
                        V.tensor_tensor(gate_a[:], ps_gate[:], ads[:].to_broadcast([P, 4, H]), ALU.add).then_inc(a_mg, 1)
                        dve.wait_ge(a_mg, q + (PAIRS + 1))
                        V.tensor_tensor(msg[:, :, 0:H], gate_a[:], hmc[:], ALU.mult).then_inc(a_msg, 1)

                either(dve, few, lambda: dve.sem_inc(s_tot, 1), all_edges)

                dve.wait_ge(s_back, 64)
                link(V.tensor_tensor(part[:, 0], part[:, 0], part[:, 1], ALU.add))
                link(V.tensor_tensor(part[:, 2], part[:, 2], part[:, 3], ALU.add))
                link(V.tensor_tensor(part[:, 0], part[:, 0], part[:, 2], ALU.add))
                dve.wait_ge(s_tot, 1)
                link(V.tensor_tensor(tot[:], tot[:], part[:, 0, :, H:H + 1], ALU.add))
                link(V.tensor_scalar(row[:], tot[:], 1e-8, None, ALU.max))
                link(V.reciprocal(row2[:], row[:]))
                link(V.tensor_tensor(tmp[:], part[:, 0, :, 0:H], row2[:].to_broadcast([P, TILES, H]), ALU.mult))
                link(V.tensor_tensor(tmp[:], tmp[:], hs_n[:], ALU.add))
                layernorm(dve, acc[:], tmp, rstd, (gam, bet))
                link(V.tensor_tensor(xs[:], xs[:], acc[:], ALU.add))
                link(V.tensor_copy(tmp[:], xs[:]))
                layernorm(dve, hs_n[:], tmp, rstd)

        with ExitStack() as st:
            stage[0] = st
            x0s = sb("x0s1", [P, TILES, H])
            acc = sb("acc1", [P, TILES, H])

            ring = sb("ring", [P, RING, TILES * P], F8)
            u_hl = sb("u_hl", [P, 2, TILES, 2 * H], F16)
            low_sum = sb("low_sum", [P, 2, 4, H])
            t_sb = sb("t_sb", [P, 4, H])
            ps_u = [pb(f"ps_u{k}", [P, 4, 2 * H]) for k in range(2)]

            part = sb("part1", [P, 4, TILES, H])
            zero = sb("zero1", [P, (ROWS // P) * W])
            gi_s = sb("gi_s1", [P, 4], I32)
            seg = sb("seg1", [P, 4])
            ug = sb("ug", [P, 4, H])
            same = sb("same1", [P, 4, P])
            before = sb("before1", [P, 4, P])
            nbef = sb("nbef1", [P, 4])
            away = sb("away1", [P, 4])
            sidx = sb("sidx1", [P, 4], I32)
            outrow = sb("outrow1", [P, 4, W])
            ps_seg = pb("ps_seg1", [P, 4, P])
            ps_sum = pb("ps_sum1", [P, 4, H + 1])
            bufs = (gi_s, None, seg, same, before, nbef, away, sidx[:], ps_seg)
            L1PASSES = STEPS + 1
            ROUNDS = TILES // RING
            PARTS = ((0, 4), (4, 3))
            block = st.enter_context(nc.Block())

            @block.sync
            def _(sp):
                def with_matrix():
                    def load_round(it, r, first):
                        for j in range(RING):
                            if not first:
                                sp.wait_ge(d_free, r * RING + (it * TILES - RING + 1 + j))
                                sp.sem_inc(s_go, 1)
                            at = slice(j, j + 1) if first else bass.ds(r * RING + j, 1)
                            sp.dma_start(ring[:, j, :].bitcast(U8), counts_d[at].rearrange("b p c -> p (b c)")).then_inc(d_in[j], 16)
                    load_round(0, 0, True)
                    for it in range(STEPS):
                        with sp.Fori(0 if it else 1, ROUNDS) as r:
                            load_round(it, r, False)

                def over_edges():
                    for p in range(L1PASSES):
                        sp.wait_ge(b_add[p], 64 * (QUADS + 1))
                        for r in range(4):
                            sp.dma_start(part[:, r], tiles(sums[r][0:NPAD, 0:H])).then_inc(b_back, 16)
                        sp.wait_ge(b_used, p + 1)
                        sp.dma_start(tiles(u_tab[:, :]), acc[:]).then_inc(b_u, 16)
                    sp.wait_ge(b_u, 16 * L1PASSES)

                either(sp, dense, with_matrix, over_edges)
                sp.wait_ge(s_fin, 1)
                sp.dma_start(tiles(out), xs[:]).then_inc(s_outd, 16)
                sp.wait_ge(s_outd, 16)

            @block.gpsimd
            def _(pool):
                def over_edges():
                    pool.wait_ge(s_zero, 3)
                    for p in range(L1PASSES):
                        zero_sums(pool, zero, b_add[p])
                        with pool.Fori(0, QUADS) as q:
                            n = q + p * QUADS
                            pool.wait_ge(b_idx, n + 1)
                            pool.sem_inc(s_mark, 1)
                            for c in range(4):
                                pool.indirect_dma_start(ug[:, c, :], None, u_tab[:, :],
                                                        bass.IndirectOffsetOnAxis(ap=gi_s[:, c:c + 1], axis=0)).then_inc(b_gath[p], 16)
                            pool.wait_ge(b_out, n + 1)
                            pool.sem_inc(s_mark, 1)
                            for c in range(4):
                                pool.indirect_dma_start(sums[c][:, :], bass.IndirectOffsetOnAxis(ap=sidx[:, c:c + 1], axis=0),
                                                        outrow[:, c, :], None, compute_op=ALU.add).then_inc(b_add[p], 16)
                        pool.wait_ge(b_u, (p + 1) * 16)

                either(pool, dense, lambda: pool.sem_inc(s_mark, 1), over_edges)

            @block.scalar
            def _(act):
                def with_matrix():
                    act.wait_ge(d_sq, 1)
                    nc.scalar.activation(dinv[:], deg[:], ACT.Sqrt).then_inc(d_ac, 1)
                    with act.Fori(0, STEPS * ROUNDS) as n:
                        for k, (j0, nj) in enumerate(PARTS):
                            act.wait_ge(d_free, n * RING + (j0 + nj))
                            nc.scalar.activation(low_sum[:, k, 0:nj, :], ps_u[k][:, 0:nj, H:2 * H], ACT.Copy).then_inc(d_lo[k], 1)

                def over_edges():
                    with act.Fori(0, QUADS) as q:
                        act.wait_ge(b_sum, q + 1)
                        nc.scalar.activation(outrow[:, :, 0:H], ps_sum[:, :, 0:H], ACT.Copy).then_inc(b_out, 1)
                    act.wait_ge(d_sq, 1)
                    nc.scalar.activation(dinv[:], deg[:], ACT.Sqrt).then_inc(d_ac, 1)
                    with act.Fori(QUADS, L1PASSES * QUADS) as n:
                        act.wait_ge(b_sum, n + 1)
                        nc.scalar.activation(outrow[:, :, 0:H], ps_sum[:, :, 0:H], ACT.Copy).then_inc(b_out, 1)

                either(act, dense, with_matrix, over_edges)

            @block.tensor
            def _(pe):
                def with_matrix():
                    for it in range(STEPS):
                        pe.wait_ge(d_u, it + 1)
                        with pe.Fori(0, ROUNDS) as r:
                            n = r + it * ROUNDS
                            for k, (j0, nj) in enumerate(PARTS):
                                pe.wait_ge(d_bank[k], n + 1)
                                for j in range(j0, j0 + nj):
                                    pe.wait_ge(d_in[j], n * 16 + 16)
                                    pe.sem_inc(d_turn, 1)
                                    for t in range(TILES):
                                        last = nc.tensor.matmul(ps_u[k][:, j - j0, :], ring[:, j, t * P:(t + 1) * P],
                                                                u_hl[:, it % 2, t, :], start=(t == 0), stop=(t == TILES - 1))
                                    last.then_inc(d_free, 1)

                def over_edges():
                    for p in range(L1PASSES):
                        with pe.Fori(0, QUADS) as q:
                            n = q + p * QUADS
                            ids_across(pe, ps_seg, seg, b_idx, n + 1, b_seg)
                            pe.wait_ge(b_eq, n + 1)
                            pe.wait_ge(b_gath[p], 64 * q + 64)
                            for c in range(4):
                                last = nc.tensor.matmul(ps_sum[:, c, 0:H], same[:, c, :], ug[:, c, :], start=True, stop=True)
                            last.then_inc(b_sum, 1)

                either(pe, dense, with_matrix, over_edges)

            @block.vector
            def _(dve):
                V = nc.vector
                link = lambda ins: dve_link(dve, ins)
                V.memset(zero[:], 0.0).then_inc(s_zero, 1)
                link(V.memset(outrow[:], 0.0))
                linked = count[0]

                def start(scale):
                    link(V.tensor_scalar(deg[:], deg[:], 1.0, None, ALU.add))
                    link(V.reciprocal(fifth[:], deg[:]))
                    link(V.tensor_scalar(fifth[:], fifth[:], 1.0 - ALPHA, None, ALU.mult))
                    dve.sem_inc(d_sq, 1)
                    dve.wait_ge(d_ac, 1)
                    link(V.reciprocal(row[:], dinv[:]))
                    link(V.tensor_copy(dinv[:], row[:]))
                    link(V.tensor_scalar(row[:], row[:], scale, None, ALU.mult))
                    link(V.tensor_tensor(acc[:], hs_n[:], row[:].to_broadcast([P, TILES, H]), ALU.mult))

                def finish(scale):
                    link(V.tensor_tensor(row[:], deg[:], dinv[:], ALU.mult))
                    link(V.tensor_scalar(row[:], row[:], 1.0 / scale, None, ALU.mult))
                    link(V.tensor_tensor(acc[:], acc[:], row[:].to_broadcast([P, TILES, H]), ALU.mult))
                    V.tensor_tensor(xs[:], xs[:], acc[:], ALU.add).then_inc(s_fin, 1)

                def with_matrix():
                    start(SCALE)
                    link(V.tensor_scalar(x0s[:], acc[:], ALPHA, None, ALU.mult))
                    link(V.tensor_copy(u_hl[:, 0, :, 0:H], acc[:]))
                    V.tensor_tensor(u_hl[:, 0, :, H:2 * H], acc[:], u_hl[:, 0, :, 0:H], ALU.subtract).then_inc(d_u, 1)
                    for k in range(2):
                        dve.sem_inc(d_bank[k], 1)
                    for it in range(STEPS):
                        with dve.Fori(0, ROUNDS) as r:
                            n = r + it * ROUNDS
                            for k, (j0, nj) in enumerate(PARTS):
                                c0 = (n * 2 + k) * 5
                                b = dve.snap(r * RING + j0)
                                own, t_ = acc[:, bass.ds(b, nj), :], t_sb[:, 0:nj, :]
                                hi, lo = (u_hl[:, (it + 1) % 2, bass.ds(b, nj), c * H:(c + 1) * H] for c in range(2))
                                dve.wait_ge(d_lo[k], n + 1)
                                V.tensor_tensor(t_, ps_u[k][:, 0:nj, 0:H], low_sum[:, k, 0:nj, :], ALU.add).then_inc(d_bank[k], 1)
                                dve.wait_ge(d_bank[k], n + 2)
                                V.tensor_tensor(t_, t_, own, ALU.add).then_inc(d_dve, 1)
                                dve.wait_ge(d_dve, c0 + 1)
                                V.tensor_tensor(t_, t_, fifth[:, bass.ds(b, nj), :].to_broadcast([P, nj, H]), ALU.mult).then_inc(d_dve, 1)
                                dve.wait_ge(d_dve, c0 + 2)
                                V.tensor_tensor(own, t_, x0s[:, bass.ds(b, nj), :], ALU.add).then_inc(d_dve, 1)
                                dve.wait_ge(d_dve, c0 + 3)
                                V.tensor_copy(hi, own).then_inc(d_dve, 1)
                                dve.wait_ge(d_dve, c0 + 4)
                                V.tensor_tensor(lo, own, hi, ALU.subtract).then_inc(d_dve, 1)
                        dve.wait_ge(d_dve, (it + 1) * ROUNDS * 10)
                        dve.sem_inc(d_u, 1)
                    finish(SCALE)

                def over_edges():
                    count[0] = linked

                    def edge_pass(p):
                        with dve.Fori(0, QUADS) as q:
                            n = q + p * QUADS
                            col = dve.snap(q * 4)
                            gather_ids(dve, bufs, b_add[p], q * 64 + 64, col, False, dst_f, b_idx)
                            merge(dve, bufs, b_seg, n, b_dve, n * 4, b_idx, b_eq)
                        dve.wait_ge(b_back, 64 * (p + 1))
                        link(V.tensor_tensor(part[:, 0], part[:, 0], part[:, 1], ALU.add))
                        link(V.tensor_tensor(part[:, 2], part[:, 2], part[:, 3], ALU.add))
                        link(V.tensor_tensor(part[:, 0], part[:, 0], part[:, 2], ALU.add))

                    edge_pass(0)
                    link(V.tensor_copy(deg[:], part[:, 0, :, 0:1]))
                    start(1.0)
                    V.tensor_scalar(x0s[:], acc[:], ALPHA, None, ALU.mult).then_inc(b_used, 1)
                    for p in range(1, L1PASSES):
                        edge_pass(p)
                        dve.wait_ge(b_u, 16 * p)
                        link(V.tensor_tensor(acc[:], acc[:], part[:, 0], ALU.add))
                        link(V.tensor_tensor(acc[:], acc[:], fifth[:].to_broadcast([P, TILES, H]), ALU.mult))
                        V.tensor_tensor(acc[:], acc[:], x0s[:], ALU.add).then_inc(b_used, 1)
                    dve.wait_ge(b_used, L1PASSES)
                    dve.wait_ge(b_u, 16 * L1PASSES)
                    finish(1.0)

                either(dve, dense, with_matrix, over_edges)


def kernel(x, src, dst, edge_attr_40, edge_weight, node_type_119, node_vec, L0_gnn_W1, L0_gnn_b1, L0_gnn_W2,
           L0_gnn_b2, L0_gnn_emb, L0_gnn_adaptW, L0_gnn_gamma, L0_gnn_beta):
    import numpy as np
    import concourse.bacc as bacc
    from concourse.bass_utils import run_bass_kernel_spmd

    def padded(a, n, value=0):
        a = np.asarray(a)
        return np.concatenate([a, np.full((n - a.shape[0],) + a.shape[1:], value, a.dtype)])

    def by_chunk(a):
        return np.ascontiguousarray(a.reshape(CHUNKS, P).T)

    fill = np.arange(EPAD - E)
    src, dst = (np.concatenate([np.asarray(a), (N + f).astype(np.asarray(a).dtype)])
                for a, f in ((src, fill % (NPAD - N)), (dst, fill * (NPAD - N) // fill.size)))

    arrays = {
        "x": padded(x, NPAD),
        "src": by_chunk(src),
        "dst": by_chunk(dst),
        "dist": by_chunk(padded(edge_weight, EPAD, 2 * CUTOFF)),
        "attr": padded(edge_attr_40, EPAD),
        "attr_t": np.ascontiguousarray(padded(edge_attr_40, EPAD).T),
        "mult_n": np.ascontiguousarray(padded(node_vec, NPAD).reshape(TILES, P).T),
        "types": padded(node_type_119, NPAD),
        "w1t": np.ascontiguousarray(np.asarray(L0_gnn_W1).T),
        "b1": np.asarray(L0_gnn_b1).reshape(H, 1),
        "w2e": np.concatenate([np.asarray(L0_gnn_W2).T, np.asarray(L0_gnn_b2).reshape(1, H)]),
        "emb": np.asarray(L0_gnn_emb),
        "emb_t": np.ascontiguousarray(np.asarray(L0_gnn_emb).T),
        "adapt_t": np.ascontiguousarray(np.asarray(L0_gnn_adaptW).T),
        "gamma": np.asarray(L0_gnn_gamma),
        "beta": np.asarray(L0_gnn_beta),
        "edge_rows": np.concatenate([padded(src, EROWS * RE).reshape(EROWS, RE),
                                     padded(dst, EROWS * RE, 2 * NPAD).reshape(EROWS, RE)], axis=1),
        "dst_first": dst[::RE],
    }
    nc = bacc.Bacc("TRN2", target_bir_lowering=False, num_devices=1)
    maps = {f"in_{n}": np.ascontiguousarray(a) for n, a in arrays.items()}
    args = [nc.dram_tensor(f"in_{n}", a.shape, mybir.dt.from_np(a.dtype), kind="ExternalInput").ap() for n, a in arrays.items()]
    out = nc.dram_tensor("out_0", (NPAD, H), F32, kind="ExternalOutput").ap()
    gnn_kernel(nc, *args, out)
    r = run_bass_kernel_spmd(nc, [maps], core_ids=[0])
    return r.results[0]["out_0"][:N]
```
